# Optimizing a Trainium2 kernel written in Bass

```python
import numpy as np
import jax
import jax.numpy as jnp

def _softmax(x, axis=-1):
    return jax.nn.softmax(x, axis=axis)

def _gelu(x):
    return jax.nn.gelu(x, approximate=True)

def _silu(x):
    return jax.nn.silu(x)

def _sigmoid(x):
    return jax.nn.sigmoid(x)

def _layernorm(x, axis=-1, eps=1e-05):
    m = jnp.mean(x, axis=axis, keepdims=True)
    v = jnp.var(x, axis=axis, keepdims=True)
    return (x - m) / jnp.sqrt(v + eps)

def _scatter_add(tgt, idx, src, axis=0):
    return tgt.at[idx].add(src)

def _segment_sum(src, seg, n):
    return jax.ops.segment_sum(src, seg, n)
kernel_name = 'mk_adj_preln_d2_adj_r2_7ff8a7'

def setup_inputs(seed: int=0):
    np.random.seed(seed)
    _w = jnp.asarray

    def _rec_inputs():
        import jax
        import jax.numpy as jnp
        _gk = jax.random.key(seed)
        x = -0.0002928 + 1 * jax.random.normal(jax.random.fold_in(_gk, 1), (128, 128, 256), jnp.float32)
        _a = jax.random.bernoulli(jax.random.fold_in(_gk, 2), 0.0625, (128, 128, 128))
        _a = jnp.logical_or(_a, jnp.swapaxes(_a, -1, -2))
        _a = jnp.logical_or(_a, jnp.eye(128, dtype=bool))
        _af = _a.astype(jnp.float32)
        _af = _af * jax.random.uniform(jax.random.fold_in(_gk, 3), (128, 128, 128), jnp.float32, 0.05, 1)
        adj = _af
        return (x, adj)
    x, adj = _rec_inputs()

    def _L0_gnn_setup():
        import jax, jax.numpy as jnp
        import numpy as np
        B, N, DIN, DOUT, K = (4, 1024, 256, 256, 3)
        key = jax.random.key(seed)
        ks = jax.random.split(key, 8)
        X = jax.random.normal(ks[0], (B, N, DIN), dtype=jnp.float32)
        A = jax.random.uniform(ks[1], (B, N, N), dtype=jnp.float32)
        Wv = jax.random.normal(ks[2], (DIN, DOUT), dtype=jnp.float32) * 0.02
        bv = jax.random.normal(ks[3], (DOUT,), dtype=jnp.float32) * 0.02
        aw = jax.random.normal(ks[4], (2 * DOUT, 1), dtype=jnp.float32) * 0.05
        ab = jax.random.normal(ks[5], (1,), dtype=jnp.float32) * 0.05
        Wk = jax.random.normal(ks[6], (K, DIN, DOUT), dtype=jnp.float32) * 0.02
        bk = jax.random.normal(ks[7], (K, DOUT), dtype=jnp.float32) * 0.02
        return {'X': X, 'A': A, 'Wv': Wv, 'bv': bv, 'aw': aw, 'ab': ab, 'Wk': Wk, 'bk': bk}
    _L0_gnn_all = _L0_gnn_setup()
    _L0_gnn_in = {k: v for k, v in _L0_gnn_all.items() if k in ('Wv', 'bv', 'aw', 'ab', 'Wk', 'bk')}
    del _L0_gnn_all

    def _L1_gnn_setup():
        import jax, jax.numpy as jnp
        import numpy as np
        B, N, F_IN, F_HID, F_OUT = (32, 512, 256, 256, 256)

        def _gcn_layer(x, adj, W, b):
            support = jnp.einsum('bnf,fh->bnh', x, W)
            return jnp.einsum('bnm,bmh->bnh', adj, support) + b
        key = jax.random.key(seed)
        ks = jax.random.split(key, 8)

        def xavier(k, fan_in, fan_out):
            bound = float(np.sqrt(6.0 / (fan_in + fan_out)))
            return jax.random.uniform(k, (fan_in, fan_out), jnp.float32, -bound, bound)
        return {'batch_graph': jax.random.normal(ks[0], (B, N, F_IN), jnp.float32), 'adj': jax.random.uniform(ks[1], (B, N, N), jnp.float32), 'W1': xavier(ks[2], F_IN, F_HID), 'b1': jnp.zeros((F_HID,), jnp.float32), 'W2': xavier(ks[3], F_HID, F_HID), 'b2': jnp.zeros((F_HID,), jnp.float32), 'W3': xavier(ks[4], F_HID, F_OUT), 'b3': jnp.zeros((F_OUT,), jnp.float32)}
    _L1_gnn_all = _L1_gnn_setup()
    _L1_gnn_in = {k: v for k, v in _L1_gnn_all.items() if k in ('W1', 'b1', 'W2', 'b2', 'W3', 'b3')}
    del _L1_gnn_all
    return {'x': x, 'adj': adj, 'L0_gnn_Wv': _L0_gnn_in['Wv'], 'L0_gnn_bv': _L0_gnn_in['bv'], 'L0_gnn_aw': _L0_gnn_in['aw'], 'L0_gnn_ab': _L0_gnn_in['ab'], 'L0_gnn_Wk': _L0_gnn_in['Wk'], 'L0_gnn_bk': _L0_gnn_in['bk'], 'L1_gnn_W1': _L1_gnn_in['W1'], 'L1_gnn_b1': _L1_gnn_in['b1'], 'L1_gnn_W2': _L1_gnn_in['W2'], 'L1_gnn_b2': _L1_gnn_in['b2'], 'L1_gnn_W3': _L1_gnn_in['W3'], 'L1_gnn_b3': _L1_gnn_in['b3']}

def reference(x, adj, L0_gnn_Wv, L0_gnn_bv, L0_gnn_aw, L0_gnn_ab, L0_gnn_Wk, L0_gnn_bk, L1_gnn_W1, L1_gnn_b1, L1_gnn_W2, L1_gnn_b2, L1_gnn_W3, L1_gnn_b3):
    import jax
    import jax.numpy as jnp

    def _L0_gnn_ref(X, A, Wv, bv, aw, ab, Wk, bk):
        import jax, jax.numpy as jnp
        import numpy as np
        B, N, DIN, DOUT, K = (4, 1024, 256, 256, 3)
        d = Wv.shape[1]
        Xw = X @ Wv + bv
        sj = Xw @ aw[:d, 0]
        si = Xw @ aw[d:, 0]
        e = jax.nn.leaky_relu(sj[:, None, :] + si[:, :, None] + ab[0], negative_slope=0.2)
        alpha_matrix = A * jnp.exp(e)
        transition = alpha_matrix / (jnp.sum(alpha_matrix, axis=-1, keepdims=True) + 1e-12)
        H = jnp.zeros(X.shape[:-1] + (d,), dtype=X.dtype)
        Xk = X
        for k in range(Wk.shape[0]):
            H = H + Xk @ Wk[k] + bk[k]
            Xk = jnp.einsum('bij,bjd->bid', transition, Xk)
        return jax.nn.relu(H)

    def _L1_gnn_ref(batch_graph, adj, W1, b1, W2, b2, W3, b3):
        import jax, jax.numpy as jnp
        import numpy as np
        B, N, F_IN, F_HID, F_OUT = (32, 512, 256, 256, 256)

        def _gcn_layer(x, adj, W, b):
            support = jnp.einsum('bnf,fh->bnh', x, W)
            return jnp.einsum('bnm,bmh->bnh', adj, support) + b
        x = jax.nn.relu(_gcn_layer(batch_graph, adj, W1, b1))
        x = jax.nn.relu(_gcn_layer(x, adj, W2, b2))
        out = _gcn_layer(x, adj, W3, b3)
        return out
    h = jnp.maximum(_layernorm(x, axis=-1), 0.0)
    x = x + _L0_gnn_ref(h, adj, L0_gnn_Wv, L0_gnn_bv, L0_gnn_aw, L0_gnn_ab, L0_gnn_Wk, L0_gnn_bk)
    h = jnp.maximum(_layernorm(x, axis=-1), 0.0)
    x = x + _L1_gnn_ref(h, adj, L1_gnn_W1, L1_gnn_b1, L1_gnn_W2, L1_gnn_b2, L1_gnn_W3, L1_gnn_b3)
    return x

_drawn_inputs = setup_inputs


def setup_inputs(seed=0):
    import zlib

    import numpy as np

    out = dict(_drawn_inputs(seed))
    spreads = {'L1_gnn_b1': (0.0, 0.281), 'L1_gnn_b2': (0.0, 0.8), 'L1_gnn_b3': (0.0, 2.0)}
    factors = {'L0_gnn_Wv': 8.0, 'L0_gnn_bv': 64.0, 'L0_gnn_aw': 8.0}
    for name, (base, spread) in spreads.items():
        noise = np.random.default_rng([zlib.crc32(name.encode()), seed]).standard_normal(out[name].shape)
        drawn = base * np.exp(spread * noise) if base else spread * noise
        out[name] = jnp.asarray(drawn.astype(out[name].dtype))
    for name, factor in factors.items():
        out[name] = (out[name] * factor).astype(out[name].dtype)
    return out
```

```python
from contextlib import ExitStack

import concourse.bass as bass
import concourse.mybir as mybir

F32 = mybir.dt.float32
F32R = mybir.dt.float32r
ALU = mybir.AluOpType
ACT = mybir.ActivationFunctionType

P = 128
G = 2
C = 2
D = C * P
K = 3
ROUND = 4
LAG_B, LAG_C, LAG_D = 1, 2, 3
LN_EPS = 1e-5
DIV_EPS = 1e-12
SLOPE = 0.2


def gnn_kernel(nc, x, adj, Wv, bv, aw, ab, Wk, bk, W1, b1, W2, b2, W3, b3, out):
    N_PAIRS = x.shape[0] // G
    ctx = ExitStack()
    with ctx:
        def sb(name, shape, dt=F32):
            return ctx.enter_context(nc.sbuf_tensor(name, shape, dt))

        def sem(name):
            return ctx.enter_context(nc.semaphore(name))

        def hilo(name, shape):
            return [sb(name + "_hi", shape, F32R), sb(name + "_lo", shape, F32R)]

        def plain(ap):
            return ap.bitcast(F32)

        ident = sb("ident", [P, P])
        w_raw = sb("w_raw", [P, 2 * K, C, D])
        wv_raw = sb("wv_raw", [P, C, D])
        w_p2 = hilo("w_p2", [P, C, D + 2])
        w_p01 = hilo("w_p01", [P, C, 2 * D])
        w_gcn = [hilo(f"w_gcn{n}", [P, C, D]) for n in range(K)]
        wva = sb("wva", [P, C, 2])
        aw_bc = sb("aw_bc", [P, 2, D])
        bv_bc = sb("bv_bc", [P, D])
        ab_bc = sb("ab_bc", [P, 1])
        bk_bc = sb("bk_bc", [P, K, D])
        scratch = sb("scratch", [P, 6, D])
        bva = sb("bva", [P, 2])
        half_c = sb("half_c", [P, 1])
        c_sum = sb("c_sum", [P, 2])
        bias_h = sb("bias_h", [P, G, D])
        bias_part = sb("bias_part", [P, D])
        bias_out = sb("bias_out", [P, G, D])
        bias_col = [sb(f"bias_col{n}", [P, C]) for n in range(2)]
        minus_half = sb("minus_half", [P, G])

        def slots(n, name, shape, dt=F32):
            return [sb(f"{name}{s}", shape, dt) for s in range(n)]

        def slots_hilo(n, name, shape):
            return [hilo(f"{name}{s}", shape) for s in range(n)]

        x_in = slots(4, "x_in", [P, G, D])
        adj_in = slots(4, "adj_in", [P, G, P])
        adjT = slots_hilo(4, "adjT", [P, G, P])
        x1b = slots(4, "x1b", [P, G, D])
        x_out = slots(4, "x_out", [P, G, D])
        stats = [slots(2, f"stats{n}_", [P, G, 6]) for n in range(2)]
        mv = [slots(2, f"mv{n}_", [P, G, 2]) for n in range(2)]
        veps = [slots(2, f"veps{n}_", [P, G]) for n in range(2)]
        rstd = [slots(2, f"rstd{n}_", [P, G]) for n in range(2)]
        nshift = slots(2, "nshift", [P, G])
        n0 = slots(2, "n0_", [P, G, D])
        n1 = slots(2, "n1_", [P, G, D])
        h0T = slots_hilo(2, "h0T", [P, C, G, P])
        h1T = slots_hilo(2, "h1T", [P, C, G, P])
        uv = slots(2, "uv", [P, G, 2])
        z = slots(2, "z", [P, G, P])
        e = slots(2, "e", [P, G, P])
        alpha = slots(2, "alpha", [P, G, P])
        rowsum = slots(2, "rowsum", [P, G])
        rinv = slots(2, "rinv", [P, G])
        tn = slots(2, "tn", [P, G, P])
        tT = slots_hilo(2, "tT", [P, G, P])
        p2 = slots_hilo(2, "p2_", [P, G, D])
        y1 = slots_hilo(2, "y1_", [P, G, D])
        hb = slots(2, "hb", [P, G, D])
        x1 = slots(2, "x1_", [P, G, D])
        s = [slots_hilo(1, f"s{n}_", [P, G, D])[0] for n in range(K)]
        y_full = [sb(f"y_full{n}", [P, C, G, P]) for n in range(2)]
        y = [hilo(f"y{n}_", [P, C, G, P]) for n in range(2)]

        def bank(name):
            return ctx.enter_context(nc.psum_tensor(name, [P, 512], F32))

        bank_hT = bank("bank_hT")
        bank_T = bank("bank_T")
        bank_p = ctx.enter_context(nc.psum_tensor("bank_p", [P, G, 512], F32))
        bank_p2 = ctx.enter_context(nc.psum_tensor("bank_p2", [P, G, 512], F32))
        bank_s = bank("bank_s")
        bank_z = bank("bank_z")
        hT_ps = bank_hT[:].rearrange("p (c g n) -> p c g n", c=C, g=G)
        T_ps = bank_T[:, 0:G * P].rearrange("p (g n) -> p g n", g=G)
        p0_ps = bank_p[:, :, 0:D]
        p1_ps = bank_p[:, :, D:2 * D]
        p2_ps = bank_p2[:, :, 0:D]
        uv_ps = bank_p2[:, :, D:D + 2]
        s3_ps = bank_p2[:, 0, :].rearrange("p (g d) -> p g d", g=G)
        s_ps = bank_s[:].rearrange("p (g d) -> p g d", g=G)
        z1_ps = bank_p2[:, 1, :].rearrange("p (c g n) -> p c g n", c=C, g=G)
        z_ps = bank_z[:].rearrange("p (c g n) -> p c g n", c=C, g=G)
        z3_ps = bank_z[:].rearrange("p (g d) -> p g d", g=G)

        consts_in, weights_in = sem("consts_in"), sem("weights_in")
        ident_zero, ident_made = sem("ident_zero"), sem("ident_made")
        exponent_made = sem("exponent_made")
        half_c_made = sem("half_c_made")
        setup = sem("setup")
        weights_cut = sem("weights_cut")
        x_landed = [sem(f"x_landed{k}") for k in range(ROUND)]
        adj_landed = [sem(f"adj_landed{k}") for k in range(ROUND)]
        stored = [sem(f"stored{k}") for k in range(ROUND)]
        stats_made = [sem(f"stats_made{n}") for n in range(2)]
        mv_made = [sem(f"mv_made{n}") for n in range(2)]
        veps_made = [sem(f"veps_made{n}") for n in range(2)]
        rstd_made = [sem(f"rstd_made{n}") for n in range(2)]
        shift_made = sem("shift_made")
        norm_made = [sem(f"norm_made{n}") for n in range(2)]
        hT_done = [sem(f"hT_done{n}") for n in range(2)]
        hT_hi = [sem(f"hT_hi{n}") for n in range(2)]
        hT_lo = [sem(f"hT_lo{n}") for n in range(2)]
        adjT_done, adjT_hi, adjT_lo = sem("adjT_done"), sem("adjT_hi"), sem("adjT_lo")
        p01_done = sem("p01_done")
        p2_done, p2_hi, p2_lo = sem("p2_done"), sem("p2_hi"), sem("p2_lo")
        uv_made = sem("uv_made")
        spread_done = sem("spread_done")
        z_made = sem("z_made")
        leaky_made = sem("leaky_made")
        exp_made = sem("exp_made")
        alpha_made = sem("alpha_made")
        sum_guarded = sem("sum_guarded")
        rinv_made = sem("rinv_made")
        tn_made = sem("tn_made")
        tT_done, tT_hi, tT_lo = sem("tT_done"), sem("tT_hi"), sem("tT_lo")
        y1_done, y1_hi, y1_lo = sem("y1_done"), sem("y1_hi"), sem("y1_lo")
        h_done = sem("h_done")
        hb_made = sem("hb_made")
        x1_made = sem("x1_made")
        x1b_made = sem("x1b_made")
        s_done = [sem(f"s_done{n}") for n in range(K)]
        s_hi = [sem(f"s_hi{n}") for n in range(K)]
        s_lo = [sem(f"s_lo{n}") for n in range(K)]
        z_done = [sem(f"z_done{n}") for n in range(K)]
        y_full_made = [sem(f"y_full_made{n}") for n in range(2)]
        y_hi = [sem(f"y_hi{n}") for n in range(2)]
        y_lo = [sem(f"y_lo{n}") for n in range(2)]
        out_made = sem("out_made")

        def rounds(eng, one):
            for i in range(ROUND):
                one(i, i)
            with eng.Fori(1, N_PAIRS // ROUND - 1) as turn:
                for k in range(ROUND):
                    one(turn * ROUND + k, k)
            for i in range(N_PAIRS - ROUND, N_PAIRS + LAG_D):
                one(i, i % ROUND)

        def here(i, lag):
            if isinstance(i, int) and not 0 <= i - lag < N_PAIRS:
                return None
            return i - lag

        def first(i):
            return isinstance(i, int) and i == 0

        def after(i, n):
            return not isinstance(i, int) or i >= n

        def landed(i, k):
            return (i - k) * (16 // ROUND) + 16

        block = ctx.enter_context(nc.Block())

        @block.sync
        def _(sp):
            def load(i, k):
                if after(i, ROUND):
                    sp.wait_ge(x1_made, i - ROUND + 1)
                    sp.wait_ge(alpha_made, i - ROUND + 1)
                    sp.wait_ge(adjT_done, i - ROUND + 1)
                sp.dma_start(x_in[k][:], x_pairs(i)).then_inc(x_landed[k], 16)
                sp.dma_start(adj_in[k][:], adj_pairs(i)).then_inc(adj_landed[k], 16)

            def x_pairs(i):
                return x[bass.ds(i * G, G)].rearrange("g n d -> n g d")

            def adj_pairs(i):
                return adj[bass.ds(i * G, G)].rearrange("g n m -> n g m")

            def store(i, k):
                sp.wait_ge(out_made, i + 1)
                sp.dma_start(out[bass.ds(i * G, G)].rearrange("g n d -> n g d"),
                             x_out[k][:]).then_inc(stored[k], 16)

            load(0, 0)
            for n in range(C):
                sp.dma_start(wv_raw[:, n, :], Wv[n * P:(n + 1) * P, :]).then_inc(consts_in, 16)
            sp.dma_start(aw_bc[:], aw.rearrange("(h d) o -> o h d", h=2).to_broadcast([P, 2, D]))\
              .then_inc(consts_in, 16)
            sp.dma_start(bv_bc[:], bv.rearrange("(o d) -> o d", o=1).to_broadcast([P, D]))\
              .then_inc(consts_in, 16)
            sp.dma_start(ab_bc[:], ab.rearrange("(o d) -> o d", o=1).to_broadcast([P, 1]))\
              .then_inc(consts_in, 16)
            sp.dma_start(bk_bc[:], bk.rearrange("(o k) d -> o k d", o=1).to_broadcast([P, K, D]))\
              .then_inc(consts_in, 16)
            for g in range(G):
                sp.dma_start(bias_out[:, g, :], b3.rearrange("(o d) -> o d", o=1).to_broadcast([P, D]))\
                  .then_inc(consts_in, 16)
            for n, b in enumerate((b1, b2)):
                sp.dma_start(bias_col[n][:], b.rearrange("(c p) -> p c", p=P),
                             allow_slow_non_contiguous=True).then_inc(consts_in, 16)
            load(1, 1)

            def one(i, k):
                if (n := here(i, -2)) is not None:
                    load(n, (k + 2) % ROUND)
                if (n := here(i, LAG_D)) is not None:
                    store(n, (k - LAG_D) % ROUND)

            rounds(sp, one)
            for k in range(ROUND):
                sp.wait_ge(stored[k], 16 * (N_PAIRS // ROUND))

        @block.gpsimd
        def _(pool):
            pool.memset(ident[:], 0.0).then_inc(ident_zero, 1)
            pool.memset(minus_half[:], -0.5).then_inc(exponent_made, 1)
            pool.wait_ge(ident_zero, 1)
            pool.affine_select(out=ident[:], in_=ident[:], compare_op=ALU.not_equal, fill=1.0, base=0,
                               pattern=[[-1, P]], channel_multiplier=1).then_inc(ident_made, 1)
            pool.wait_ge(exponent_made, 1)

            def power(n, i, k):
                pool.wait_ge(veps_made[n], i + 1)
                if after(i, 2):
                    pool.wait_ge(norm_made[n], i - 1)
                pool.tensor_tensor(rstd[n][k % 2][:], veps[n][k % 2][:], minus_half[:], ALU.pow)\
                    .then_inc(rstd_made[n], 1)

            def y_low(n, i, k):
                pool.wait_ge(y_hi[n], i + 1)
                if after(i, 1):
                    pool.wait_ge(s_done[n + 1], i)
                pool.tensor_tensor(y[n][1][:], y_full[n][:], plain(y[n][0][:]), ALU.subtract)\
                    .then_inc(y_lo[n], 1)

            def out_bias(i, k):
                pool.wait_ge(x1_made, i + 1)
                if first(i):
                    pool.wait_ge(consts_in, 16 * (C + 8))
                if after(i, 4):
                    pool.wait_ge(out_made, i - 3)
                pool.tensor_tensor(x1b[k][:], x1[k % 2][:], bias_out[:], ALU.add).then_inc(x1b_made, 1)

            power(0, 0, 0)

            def one(i, k):
                b, c = here(i, LAG_B), here(i, LAG_C)
                if c is not None:
                    y_low(0, c, k - LAG_C)
                if b is not None:
                    power(1, b, k - LAG_B)
                    out_bias(b, (k - LAG_B) % ROUND)
                if (n := here(i, -1)) is not None:
                    power(0, n, k + 1)
                if c is not None:
                    y_low(1, c, k - LAG_C)

            rounds(pool, one)

        @block.scalar
        def _(act):
            for n, w in enumerate((Wk[0], Wk[1], Wk[2], W1, W2, W3)):
                act.dma_start(w_raw[:, n, :, :], w.rearrange("(c p) d -> p c d", p=P))\
                   .then_inc(weights_in, 16)

            def hT_high(n, i, k):
                act.wait_ge(hT_done[n], i + 1)
                if after(i, 2):
                    act.wait_ge((p01_done, s_done[0])[n], i - 1)
                act.activation((h0T, h1T)[n][k % 2][0][:], hT_ps, ACT.Relu).then_inc(hT_hi[n], 1)

            def adjT_high(i, k):
                act.wait_ge(adjT_done, i + 1)
                if after(i, 4):
                    act.wait_ge(z_done[2], i - 3)
                act.activation(adjT[k % 4][0][:], T_ps, ACT.Copy).then_inc(adjT_hi, 1)

            def scores_copy(i, k):
                act.wait_ge(p2_done, i + 1)
                if first(i):
                    act.wait_ge(half_c_made, 1)
                if after(i, 2):
                    act.wait_ge(spread_done, i - 1)
                    act.wait_ge(z_made, i - 1)
                act.activation(uv[k % 2][:], uv_ps, ACT.Identity, bias=half_c[:]).then_inc(uv_made, 1)

            def p2_high(i, k):
                if after(i, 2):
                    act.wait_ge(y1_done, i - 1)
                act.activation(p2[k % 2][0][:], p2_ps, ACT.Copy).then_inc(p2_hi, 1)

            def logits(i, k):
                act.wait_ge(spread_done, i + 1)
                act.wait_ge(uv_made, i + 1)
                if after(i, 2):
                    act.wait_ge(exp_made, i - 1)
                act.activation(z[k % 2][:, 0, :], T_ps[:, 0, :], ACT.Identity, bias=uv[k % 2][:, 0, 1:2])
                act.activation(z[k % 2][:, 1, :], T_ps[:, 1, :], ACT.Identity, bias=uv[k % 2][:, 1, 1:2])\
                   .then_inc(z_made, 1)

            def exponentials(i, k):
                act.wait_ge(leaky_made, i + 1)
                if after(i, 2):
                    act.wait_ge(alpha_made, i - 1)
                act.activation(e[k % 2][:], z[k % 2][:], ACT.Exp).then_inc(exp_made, 1)

            def tT_high(i, k):
                act.wait_ge(tT_done, i + 1)
                if after(i, 2):
                    act.wait_ge(h_done, i - 1)
                act.activation(tT[k % 2][0][:], T_ps, ACT.Copy).then_inc(tT_hi, 1)

            def y1_high(i, k):
                act.wait_ge(y1_done, i + 1)
                if after(i, 2):
                    act.wait_ge(h_done, i - 1)
                act.activation(y1[k % 2][0][:], p1_ps, ACT.Copy).then_inc(y1_hi, 1)

            def norm(i, k):
                act.wait_ge(shift_made, i + 1)
                if after(i, 2):
                    act.wait_ge(hT_done[1], i - 1)
                for g in range(G):
                    last = act.activation(n1[k % 2][:, g, :], x1[k % 2][:, g, :], ACT.Identity,
                                          bias=nshift[k % 2][:, g:g + 1], scale=rstd[1][k % 2][:, g:g + 1])
                last.then_inc(norm_made[1], 1)

            def s_high(n, i):
                act.wait_ge(s_done[n], i + 1)
                if after(i, 1):
                    act.wait_ge(z_done[n], i)
                act.activation(s[n][0][:], (s_ps, s_ps, s3_ps)[n], ACT.Copy).then_inc(s_hi[n], 1)

            def y_high(n, i):
                z_in = (z1_ps, z_ps)[n]
                act.wait_ge(z_done[n], i + 1)
                if first(i):
                    act.wait_ge(consts_in, 16 * (C + 8))
                if after(i, 1):
                    act.wait_ge(y_lo[n], i)
                    act.wait_ge(s_done[n + 1], i)
                for c in range(C):
                    act.activation(y_full[n][:, c], z_in[:, c], ACT.Relu, bias=bias_col[n][:, c:c + 1])
                for c in range(C):
                    last = act.activation(y[n][0][:, c], z_in[:, c], ACT.Relu, bias=bias_col[n][:, c:c + 1])
                last.then_inc(y_hi[n], 1)

            def one(i, k):
                a, b, c = here(i, 0), here(i, LAG_B), here(i, LAG_C)
                if a is not None:
                    hT_high(0, a, k)
                    adjT_high(a, k)
                if c is not None:
                    y_high(0, c)
                if a is not None:
                    scores_copy(a, k)
                    p2_high(a, k)
                if c is not None:
                    s_high(1, c)
                if a is not None:
                    logits(a, k)
                if b is not None:
                    norm(b, k - LAG_B)
                if a is not None:
                    exponentials(a, k)
                if b is not None:
                    hT_high(1, b, k - LAG_B)
                if c is not None:
                    y_high(1, c)
                if b is not None:
                    s_high(0, b)
                if a is not None:
                    tT_high(a, k)
                if c is not None:
                    s_high(2, c)
                if a is not None:
                    y1_high(a, k)

            rounds(act, one)

        CUTS = 2 * (1 + 3 + K)

        @block.vector
        def _(dve):
            def low(dst, src, hi, signal):
                dve.tensor_tensor(dst, src, plain(hi), ALU.subtract).then_inc(signal, 1)

            def statistics(n, i, k, src):
                if after(i, 2):
                    dve.wait_ge(mv_made[n], i - 1)
                for g in range(G):
                    last = dve.bn_stats(stats[n][k % 2][:, g, :], src[:, g, :])
                last.then_inc(stats_made[n], 1)

            def moments(n, i, k, between):
                dve.wait_ge(stats_made[n], i + 1)
                if after(i, 2):
                    dve.wait_ge((norm_made[0], shift_made)[n], i - 1)
                between()
                for g in range(G):
                    last = dve.bn_aggr(mv[n][k % 2][:, g, :], stats[n][k % 2][:, g, :])
                last.then_inc(mv_made[n], 1)

            def guard_variance(n, i, k):
                dve.wait_ge(mv_made[n], i + 1)
                if after(i, 2):
                    dve.wait_ge(rstd_made[n], i - 1)
                dve.tensor_scalar(veps[n][k % 2][:], mv[n][k % 2][:, :, 1], LN_EPS, None, ALU.add)\
                   .then_inc(veps_made[n], 1)

            def x_statistics(i, k):
                dve.wait_ge(x_landed[k], landed(i, k))
                statistics(0, i, k, x_in[k])

            def x_norm(i, k):
                dve.wait_ge(rstd_made[0], i + 1)
                if after(i, 2):
                    dve.wait_ge(hT_done[0], i - 1)
                for g in range(G):
                    last = dve.tensor_scalar(n0[k % 2][:, g, :], x_in[k][:, g, :], mv[0][k % 2][:, g, 0:1],
                                             rstd[0][k % 2][:, g:g + 1], ALU.subtract, ALU.mult)
                last.then_inc(norm_made[0], 1)

            def shift(i, k):
                dve.wait_ge(rstd_made[1], i + 1)
                if after(i, 2):
                    dve.wait_ge(norm_made[1], i - 1)
                dve.scalar_tensor_tensor(nshift[k % 2][:], mv[1][k % 2][:, :, 0], -1.0, rstd[1][k % 2][:],
                                         ALU.mult, ALU.mult).then_inc(shift_made, 1)

            def hT_low(n, i, k):
                hi, lo = (h0T, h1T)[n][k % 2]
                dve.wait_ge(hT_hi[n], i + 1)
                if after(i, 2):
                    dve.wait_ge((p01_done, s_done[0])[n], i - 1)
                dve.scalar_tensor_tensor(lo[:], hT_ps, 0.0, plain(hi[:]), ALU.max, ALU.subtract)\
                   .then_inc(hT_lo[n], 1)

            def adjT_low(i, k):
                dve.wait_ge(adjT_hi, i + 1)
                if after(i, 4):
                    dve.wait_ge(z_done[2], i - 3)
                low(adjT[k][1][:], T_ps, adjT[k][0][:], adjT_lo)

            def p2_low(i, k):
                dve.wait_ge(p2_hi, i + 1)
                if after(i, 2):
                    dve.wait_ge(y1_done, i - 1)
                low(p2[k % 2][1][:], p2_ps, p2[k % 2][0][:], p2_lo)

            def leaky(i, k):
                dve.wait_ge(z_made, i + 1)
                zz = z[k % 2][:]
                dve.scalar_tensor_tensor(zz, zz, SLOPE, zz, ALU.mult, ALU.max).then_inc(leaky_made, 1)

            def attention(i, k):
                dve.wait_ge(exp_made, i + 1)
                dve.wait_ge(adj_landed[k], landed(i, k))
                if after(i, 2):
                    dve.wait_ge(tn_made, i - 1)
                for g in range(G):
                    last = dve.tensor_tensor_reduce(alpha[k % 2][:, g, :], adj_in[k][:, g, :],
                                                    e[k % 2][:, g, :], 1.0, 0.0, ALU.mult, ALU.add,
                                                    rowsum[k % 2][:, g:g + 1])
                last.then_inc(alpha_made, 1)

            def guard_sum(i, k):
                dve.wait_ge(alpha_made, i + 1)
                dve.tensor_scalar(rowsum[k % 2][:], rowsum[k % 2][:], DIV_EPS, None, ALU.add)\
                   .then_inc(sum_guarded, 1)

            def invert_sum(i, k):
                dve.wait_ge(sum_guarded, i + 1)
                dve.reciprocal(rinv[k % 2][:], rowsum[k % 2][:]).then_inc(rinv_made, 1)

            def transition(i, k):
                dve.wait_ge(rinv_made, i + 1)
                if after(i, 2):
                    dve.wait_ge(tT_done, i - 1)
                for g in range(G):
                    last = dve.tensor_scalar(tn[k % 2][:, g, :], alpha[k % 2][:, g, :],
                                             rinv[k % 2][:, g:g + 1], None, ALU.mult)
                last.then_inc(tn_made, 1)

            def tT_low(i, k):
                dve.wait_ge(tT_hi, i + 1)
                if after(i, 2):
                    dve.wait_ge(h_done, i - 1)
                low(tT[k % 2][1][:], T_ps, tT[k % 2][0][:], tT_lo)

            def y1_low(i, k):
                dve.wait_ge(y1_hi, i + 1)
                if after(i, 2):
                    dve.wait_ge(h_done, i - 1)
                low(y1[k % 2][1][:], p1_ps, y1[k % 2][0][:], y1_lo)

            def h_bias(i, k):
                dve.wait_ge(h_done, i + 1)
                if after(i, 2):
                    dve.wait_ge(x1_made, i - 1)
                dve.tensor_tensor(hb[k % 2][:], p0_ps, bias_h[:], ALU.add).then_inc(hb_made, 1)

            def residual(i, k):
                dve.wait_ge(hb_made, i + 1)
                if after(i, 2):
                    dve.wait_ge(x1b_made, i - 1)
                    dve.wait_ge(norm_made[1], i - 1)
                dve.scalar_tensor_tensor(x1[k % 2][:], hb[k % 2][:], 0.0, x_in[k][:], ALU.max, ALU.add)\
                   .then_inc(x1_made, 1)

            def x1_statistics(i, k):
                dve.wait_ge(x1_made, i + 1)
                statistics(1, i, k, x1[k % 2])

            def s_low(n, i):
                dve.wait_ge(s_hi[n], i + 1)
                if after(i, 1):
                    dve.wait_ge(z_done[n], i)
                low(s[n][1][:], (s_ps, s_ps, s3_ps)[n], s[n][0][:], s_lo[n])

            def finish(i, k):
                dve.wait_ge(z_done[2], i + 1)
                dve.wait_ge(x1b_made, i + 1)
                if after(i, 4):
                    dve.wait_ge(stored[k], landed(i - ROUND, k))
                dve.tensor_tensor(x_out[k][:], z3_ps, x1b[k][:], ALU.add).then_inc(out_made, 1)

            step = [0]

            def chain(ins):
                step[0] += 1
                ins.then_inc(setup, 1)
                dve.wait_ge(setup, step[0])

            x_statistics(0, 0)
            moments(0, 0, 0, lambda: None)
            guard_variance(0, 0, 0)
            dve.wait_ge(consts_in, 16 * (C + 8))
            for c in range(C):
                for h in range(2):
                    chain(dve.tensor_tensor_reduce(scratch[:, 2 * c + h, :], wv_raw[:, c, :], aw_bc[:, h, :],
                                                   1.0, 0.0, ALU.mult, ALU.add, wva[:, c, h:h + 1]))
            for h in range(2):
                chain(dve.tensor_tensor_reduce(scratch[:, 4 + h, :], bv_bc[:], aw_bc[:, h, :],
                                               1.0, 0.0, ALU.mult, ALU.add, bva[:, h:h + 1]))
            chain(dve.tensor_tensor(c_sum[:, 0:1], bva[:, 0:1], bva[:, 1:2], ALU.add))
            chain(dve.tensor_tensor(c_sum[:, 1:2], c_sum[:, 0:1], ab_bc[:], ALU.add))
            dve.tensor_scalar(half_c[:], c_sum[:, 1:2], 0.5, None, ALU.mult).then_inc(half_c_made, 1)
            chain(dve.tensor_tensor(bias_part[:], bk_bc[:, 0, :], bk_bc[:, 1, :], ALU.add))
            for g in range(G):
                chain(dve.tensor_tensor(bias_h[:, g, :], bias_part[:], bk_bc[:, 2, :], ALU.add))
            x_norm(0, 0)
            dve.wait_ge(weights_in, 16 * 2 * K)
            cuts = [(w_p2, slice(0, D), w_raw[:, 2]), (w_p2, slice(D, D + 2), wva),
                    (w_p01, slice(0, D), w_raw[:, 0]), (w_p01, slice(D, 2 * D), w_raw[:, 1]),
                    *[(w_gcn[n], slice(0, D), w_raw[:, K + n]) for n in range(K)]]
            for n, (w, cols, raw) in enumerate(cuts):
                dve.tensor_copy(w[0][:, :, cols], raw[:]).then_inc(weights_cut, 1)
                dve.wait_ge(weights_cut, 2 * n + 1)
                dve.tensor_tensor(w[1][:, :, cols], raw[:], plain(w[0][:, :, cols]), ALU.subtract)\
                   .then_inc(weights_cut, 1)

            def one(i, k):
                a, b, c, d = here(i, 0), here(i, LAG_B), here(i, LAG_C), here(i, LAG_D)
                nxt = here(i, -1)
                kb, kd, kn = (k - LAG_B) % ROUND, (k - LAG_D) % ROUND, (k + 1) % ROUND
                if a is not None:
                    hT_low(0, a, k)
                if b is not None:
                    h_bias(b, kb)
                if a is not None:
                    adjT_low(a, k)
                if b is not None:
                    residual(b, kb)
                if d is not None:
                    finish(d, kd)
                if b is not None:
                    x1_statistics(b, kb)
                    moments(1, b, kb, lambda: p2_low(a, k) if a is not None else None)
                    guard_variance(1, b, kb)
                elif a is not None:
                    p2_low(a, k)
                if b is not None:
                    shift(b, kb)
                if c is not None:
                    s_low(1, c)
                if a is not None:
                    leaky(a, k)
                if nxt is not None:
                    x_statistics(nxt, kn)
                if nxt is not None:
                    moments(0, nxt, kn, lambda: attention(a, k))
                elif a is not None:
                    attention(a, k)
                if a is not None:
                    guard_sum(a, k)
                    invert_sum(a, k)
                    transition(a, k)
                if nxt is not None:
                    guard_variance(0, nxt, kn)
                if b is not None:
                    hT_low(1, b, kb)
                    s_low(0, b)
                if nxt is not None:
                    x_norm(nxt, kn)
                if a is not None:
                    tT_low(a, k)
                if c is not None:
                    s_low(2, c)
                if a is not None:
                    y1_low(a, k)

            rounds(dve, one)

        @block.tensor
        def _(pe):
            HI, LO = 0, 1
            PARTS = ((HI, HI), (HI, LO), (LO, HI))

            def matmul(dst, stationary, moving, start, stop):
                return pe.matmul(dst, stationary, moving, start=start, stop=stop, skip_group_check=True)

            def turn_h(n, i, k):
                pe.wait_ge(norm_made[n], i + 1)
                if n == 0 and after(i, 2):
                    pe.wait_ge(hT_lo[1], i - 1)
                if n == 0 and isinstance(i, int) and i == 1:
                    pe.wait_ge(hT_lo[0], 1)
                if n == 1 and here(i, -1) is not None:
                    pe.wait_ge(hT_lo[0], i + 2)
                src = (n0, n1)[n][k % 2]
                for c in range(C):
                    for g in range(G):
                        last = pe.transpose(hT_ps[:, c, g, :], src[:, g, c * P:(c + 1) * P], ident[:])
                last.then_inc(hT_done[n], 1)

            def turn_adj(i, k):
                pe.wait_ge(adj_landed[k], landed(i, k))
                if after(i, 1):
                    pe.wait_ge(tT_lo, i)
                for g in range(G):
                    last = pe.transpose(T_ps[:, g, :], adj_in[k][:, g, :], ident[:])
                last.then_inc(adjT_done, 1)

            def spread_scores(i, k):
                pe.wait_ge(uv_made, i + 1)
                pe.wait_ge(adjT_lo, i + 1)
                for g in range(G):
                    last = pe.transpose(T_ps[:, g, :], uv[k % 2][:, g, 0:1].to_broadcast([P, P]), ident[:])
                last.then_inc(spread_done, 1)

            def turn_T(i, k):
                pe.wait_ge(tn_made, i + 1)
                pe.wait_ge(z_made, i + 1)
                for g in range(G):
                    last = pe.transpose(T_ps[:, g, :], tn[k % 2][:, g, :], ident[:])
                last.then_inc(tT_done, 1)

            def times_weights(hT, w, dst, starts, lo_wait):
                steps = [(g, c, a, b) for low in (False, True) for g in range(G) for c in range(C)
                         for a, b in PARTS if (a == LO) == low]
                for n, (g, c, a, b) in enumerate(steps):
                    if a == LO and steps[n - 1][2] == HI:
                        lo_wait()
                    start = c == 0 and a == HI and b == HI and g in starts
                    last = matmul(dst[g], hT[a][:, c, g, :], w[b][:, c, :], start, a == LO and c == C - 1)
                return last

            def p2_product(i, k):
                pe.wait_ge(hT_hi[0], i + 1)
                if first(i):
                    pe.wait_ge(weights_cut, CUTS)
                if after(i, 3):
                    pe.wait_ge(s_lo[2], i - 2)
                if after(i, 2):
                    pe.wait_ge(y_hi[0], i - 1)
                if after(i, 1):
                    pe.wait_ge(p2_lo, i)
                times_weights(h0T[k % 2], w_p2, [bank_p2[:, g, 0:D + 2] for g in range(G)], range(G),
                              lambda: pe.wait_ge(hT_lo[0], i + 1)).then_inc(p2_done, 1)

            def p01_product(i, k, g):
                if g == 0 and after(i, 1):
                    pe.wait_ge(hb_made, i)
                for c in range(C):
                    for a, b in PARTS:
                        last = matmul(bank_p[:, g, :], h0T[k % 2][a][:, c, g, :], w_p01[b][:, c, :],
                                      c == 0 and (a, b) == (HI, HI), c == C - 1 and a == LO)
                if g == G - 1:
                    last.then_inc(p01_done, 1)

            def times_T(dst, t, src, g, a, b):
                return matmul(dst[:, g, :], t[a][:, g, :], src[b][:, g, :], False, (a, b) == (LO, HI))

            def y1_product(i, k):
                pe.wait_ge(tT_hi, i + 1)
                pe.wait_ge(p2_lo, i + 1)
                for g in range(G):
                    for a, b in ((HI, HI), (HI, LO)):
                        times_T(p1_ps, tT[k % 2], p2[k % 2], g, a, b)
                pe.wait_ge(tT_lo, i + 1)
                for g in range(G):
                    last = times_T(p1_ps, tT[k % 2], p2[k % 2], g, LO, HI)
                last.then_inc(y1_done, 1)

            def h_product(i, k):
                pe.wait_ge(y1_lo, i + 1)
                for g in range(G):
                    for a, b in PARTS:
                        last = times_T(p0_ps, tT[k % 2], y1[k % 2], g, a, b)
                last.then_inc(h_done, 1)

            def s_product(n, i, k):
                if n == 0:
                    pe.wait_ge(hT_hi[1], i + 1)
                    if after(i, 1):
                        pe.wait_ge(s_lo[1], i)
                    times_weights(h1T[k % 2], w_gcn[0], [s_ps[:, g, :] for g in range(G)], (0,),
                                  lambda: pe.wait_ge(hT_lo[1], i + 1)).then_inc(s_done[0], 1)
                if n == 1:
                    pe.wait_ge(y_hi[0], i + 1)
                    pe.wait_ge(s_lo[0], i + 1)
                    times_weights(y[0], w_gcn[1], [s_ps[:, g, :] for g in range(G)], (0,),
                                  lambda: pe.wait_ge(y_lo[0], i + 1)).then_inc(s_done[1], 1)
                if n == 2:
                    pe.wait_ge(y_hi[1], i + 1)
                    if here(i, -LAG_C) is not None:
                        pe.wait_ge(p2_lo, i + LAG_C + 1)
                    times_weights(y[1], w_gcn[2], [s3_ps[:, g, :] for g in range(G)], (0,),
                                  lambda: pe.wait_ge(y_lo[1], i + 1)).then_inc(s_done[2], 1)

            def z_product(n, i, k):
                pe.wait_ge(s_hi[n], i + 1)
                pe.wait_ge(adjT_lo, i + 1)
                if n == 0 and here(i, -LAG_B) is not None:
                    pe.wait_ge(p2_lo, i + LAG_B + 1)
                if n == 1 and after(i, 1):
                    pe.wait_ge(out_made, i)
                dst = (z1_ps, z_ps)[n]
                steps = [(g, c, a, b) for low in (False, True) for g in range(G) for c in range(C)
                         for a, b in PARTS if (a == LO) == low]
                for m, (g, c, a, b) in enumerate(steps):
                    if a == LO and steps[m - 1][2] == HI:
                        pe.wait_ge(s_lo[n], i + 1)
                    last = matmul(dst[:, c, g, :], s[n][a][:, g, c * P:(c + 1) * P], adjT[k][b][:, g, :],
                                  m == 0, a == LO)
                last.then_inc(z_done[n], 1)

            def z3_product(i, k):
                pe.wait_ge(s_lo[2], i + 1)
                for g in range(G):
                    for a, b in PARTS:
                        last = matmul(z3_ps[:, g, :], adjT[k][a][:, g, :], s[2][b][:, g, :],
                                      g == 0 and (a, b) == (HI, HI), (a, b) == (LO, HI))
                last.then_inc(z_done[2], 1)

            pe.wait_ge(ident_made, 1)

            def one(i, k):
                a, b, c, d = here(i, 0), here(i, LAG_B), here(i, LAG_C), here(i, LAG_D)
                kb, kc, kd = (k - LAG_B) % ROUND, (k - LAG_C) % ROUND, (k - LAG_D) % ROUND
                if a is not None:
                    turn_h(0, a, k)
                    turn_adj(a, k)
                if b is not None:
                    h_product(b, kb)
                if d is not None:
                    z3_product(d, kd)
                if a is not None:
                    p2_product(a, k)
                if c is not None:
                    s_product(1, c, kc)
                if a is not None:
                    spread_scores(a, k)
                    p01_product(a, k, 0)
                if c is not None:
                    z_product(1, c, kc)
                if b is not None:
                    turn_h(1, b, kb)
                if a is not None:
                    p01_product(a, k, 1)
                if b is not None:
                    s_product(0, b, kb)
                if a is not None:
                    turn_T(a, k)
                if c is not None:
                    s_product(2, c, kc)
                if a is not None:
                    y1_product(a, k)
                if b is not None:
                    z_product(0, b, kb)

            rounds(pe, one)


_OUT = "x_new"


def kernel(**inputs):
    import numpy as np
    import concourse.bacc as bacc
    from concourse.bass_utils import run_bass_kernel_spmd

    nc = bacc.Bacc("TRN2", target_bir_lowering=False, num_devices=1)
    arrays, args = {}, []
    for name in ("x", "adj", *("L0_gnn_" + n for n in ("Wv", "bv", "aw", "ab", "Wk", "bk")),
                 *("L1_gnn_" + n for n in ("W1", "b1", "W2", "b2", "W3", "b3"))):
        a = np.ascontiguousarray(inputs[name])
        arrays["in_" + name] = a
        args.append(nc.dram_tensor("in_" + name, a.shape, mybir.dt.from_np(a.dtype), kind="ExternalInput").ap())
    args.append(nc.dram_tensor(_OUT, inputs["x"].shape, F32, kind="ExternalOutput").ap())
    gnn_kernel(nc, *args)
    return run_bass_kernel_spmd(nc, [arrays], core_ids=[0]).results[0][_OUT]
```

```python
from contextlib import ExitStack

import concourse.bass as bass
import concourse.mybir as mybir

F32 = mybir.dt.float32
F32R = mybir.dt.float32r
ALU = mybir.AluOpType
ACT = mybir.ActivationFunctionType

P = 128
G = 2
C = 2
D = C * P
K = 3
ROUND = 4
LAG_B, LAG_C, LAG_D = 1, 2, 3
LN_EPS = 1e-5
DIV_EPS = 1e-12
SLOPE = 0.2


def gnn_kernel(nc, x, adj, Wv, bv, aw, ab, Wk, bk, W1, b1, W2, b2, W3, b3, out):
    N_PAIRS = x.shape[0] // G
    ctx = ExitStack()
    with ctx:
        def sb(name, shape, dt=F32):
            return ctx.enter_context(nc.sbuf_tensor(name, shape, dt))

        def sem(name):
            return ctx.enter_context(nc.semaphore(name))

        def hilo(name, shape):
            return [sb(name + "_hi", shape, F32R), sb(name + "_lo", shape, F32R)]

        def plain(ap):
            return ap.bitcast(F32)

        ident = sb("ident", [P, P])
        w_raw = sb("w_raw", [P, 2 * K, C, D])
        wv_raw = sb("wv_raw", [P, C, D])
        w_p2 = hilo("w_p2", [P, C, D + 2])
        w_p01 = hilo("w_p01", [P, C, 2 * D])
        w_gcn = [hilo(f"w_gcn{n}", [P, C, D]) for n in range(K)]
        wva = sb("wva", [P, C, 2])
        aw_bc = sb("aw_bc", [P, 2, D])
        bv_bc = sb("bv_bc", [P, D])
        ab_bc = sb("ab_bc", [P, 1])
        bk_bc = sb("bk_bc", [P, K, D])
        scratch = sb("scratch", [P, 6, D])
        bva = sb("bva", [P, 2])
        half_c = sb("half_c", [P, 1])
        c_sum = sb("c_sum", [P, 2])
        bias_h = sb("bias_h", [P, G, D])
        bias_part = sb("bias_part", [P, D])
        bias_out = sb("bias_out", [P, G, D])
        bias_col = [sb(f"bias_col{n}", [P, C]) for n in range(2)]
        minus_half = sb("minus_half", [P, G])

        def slots(n, name, shape, dt=F32):
            return [sb(f"{name}{s}", shape, dt) for s in range(n)]

        def slots_hilo(n, name, shape):
            return [hilo(f"{name}{s}", shape) for s in range(n)]

        x_in = slots(4, "x_in", [P, G, D])
        adj_in = slots(4, "adj_in", [P, G, P])
        adjT_full = slots(4, "adjT_full", [P, G, P])
        adjT = slots_hilo(4, "adjT", [P, G, P])
        x1b = slots(4, "x1b", [P, G, D])
        x_out = slots(4, "x_out", [P, G, D])
        stats = [slots(2, f"stats{n}_", [P, G, 6]) for n in range(2)]
        mv = [slots(2, f"mv{n}_", [P, G, 2]) for n in range(2)]
        veps = [slots(2, f"veps{n}_", [P, G]) for n in range(2)]
        rstd = [slots(2, f"rstd{n}_", [P, G]) for n in range(2)]
        nshift = slots(2, "nshift", [P, G])
        n0 = slots(2, "n0_", [P, G, D])
        h1 = slots(2, "h1_", [P, G, D])
        h0T = slots_hilo(2, "h0T", [P, C, G, P])
        uv = slots(2, "uv", [P, G, 2])
        z = slots(2, "z", [P, G, P])
        e = slots(2, "e", [P, G, P])
        alpha = slots(2, "alpha", [P, G, P])
        rowsum = slots(2, "rowsum", [P, G])
        rinv = slots(2, "rinv", [P, G])
        tn = slots(2, "tn", [P, G, P])
        tT = slots_hilo(2, "tT", [P, G, P])
        p2 = slots_hilo(2, "p2_", [P, G, D])
        y1 = slots_hilo(2, "y1_", [P, G, D])
        hb = slots(2, "hb", [P, G, D])
        x1 = slots(2, "x1_", [P, G, D])
        m = hilo("m", [P, C, G, P])
        s2 = sb("s2", [P, G, D])
        s3 = hilo("s3", [P, G, D])
        y_full = [sb(f"y_full{n}", [P, C, G, P]) for n in range(2)]
        y = [hilo(f"y{n}_", [P, C, G, P]) for n in range(2)]

        def bank(name):
            return ctx.enter_context(nc.psum_tensor(name, [P, 512], F32))

        bank_turned = bank("bank_turned")
        bank_T = bank("bank_T")
        bank_p = ctx.enter_context(nc.psum_tensor("bank_p", [P, G, 512], F32))
        bank_p2 = ctx.enter_context(nc.psum_tensor("bank_p2", [P, G, 512], F32))
        bank_2 = bank("bank_2")
        bank_3 = bank("bank_3")
        turned_ps = bank_turned[:].rearrange("p (c g n) -> p c g n", c=C, g=G)
        T_ps = bank_T[:, 0:G * P].rearrange("p (g n) -> p g n", g=G)
        p0_ps = bank_p[:, :, 0:D]
        p1_ps = bank_p[:, :, D:2 * D]
        p2_ps = bank_p2[:, :, 0:D]
        uv_ps = bank_p2[:, :, D:D + 2]
        z1_ps = bank_2[:].rearrange("p (c g n) -> p c g n", c=C, g=G)
        s2_ps = bank_2[:].rearrange("p (g d) -> p g d", g=G)
        z2_ps = bank_2[:].rearrange("p (c g n) -> p c g n", c=C, g=G)
        s3_ps = bank_3[:].rearrange("p (g d) -> p g d", g=G)
        z3_ps = bank_3[:].rearrange("p (g d) -> p g d", g=G)

        score_weights_in = sem("score_weights_in")
        score_consts_in = sem("score_consts_in")
        biases_in = sem("biases_in")
        p2_weights_in = sem("p2_weights_in")
        p01_weights_in = sem("p01_weights_in")
        gcn_weights_in = [sem(f"gcn_weights_in{n}") for n in range(K)]
        ident_zero, ident_made = sem("ident_zero"), sem("ident_made")
        exponent_made = sem("exponent_made")
        half_c_made = sem("half_c_made")
        wva_made, bva_made, c_summed = sem("wva_made"), sem("bva_made"), sem("c_summed")
        bias_h_made = sem("bias_h_made")
        k_weights_hi = sem("k_weights_hi")
        p2_weights_cut = sem("p2_weights_cut")
        p01_weights_cut = sem("p01_weights_cut")
        gcn_weights_hi = sem("gcn_weights_hi")
        gcn_weights_cut = sem("gcn_weights_cut")
        x_landed = [sem(f"x_landed{k}") for k in range(ROUND)]
        adj_landed = [sem(f"adj_landed{k}") for k in range(ROUND)]
        stored = [sem(f"stored{k}") for k in range(ROUND)]
        stats_made = [sem(f"stats_made{n}") for n in range(2)]
        mv_made = [sem(f"mv_made{n}") for n in range(2)]
        veps_made = [sem(f"veps_made{n}") for n in range(2)]
        rstd_made = [sem(f"rstd_made{n}") for n in range(2)]
        shift_made = sem("shift_made")
        norm_made = [sem(f"norm_made{n}") for n in range(2)]
        hT_done, hT_hi, hT_lo = sem("hT_done"), sem("hT_hi"), sem("hT_lo")
        adjT_done, adjT_hi, adjT_lo = sem("adjT_done"), sem("adjT_hi"), sem("adjT_lo")
        p01_done = sem("p01_done")
        p2_done, p2_hi, p2_lo = sem("p2_done"), sem("p2_hi"), sem("p2_lo")
        uv_made = sem("uv_made")
        spread_done = sem("spread_done")
        z_made = sem("z_made")
        leaky_made = sem("leaky_made")
        exp_made = sem("exp_made")
        alpha_made = sem("alpha_made")
        sum_guarded = sem("sum_guarded")
        rinv_made = sem("rinv_made")
        tn_made = sem("tn_made")
        tT_done, tT_hi, tT_lo = sem("tT_done"), sem("tT_hi"), sem("tT_lo")
        y1_done, y1_hi, y1_lo = sem("y1_done"), sem("y1_hi"), sem("y1_lo")
        h_done = sem("h_done")
        hb_made = sem("hb_made")
        x1_made = sem("x1_made")
        x1b_made = sem("x1b_made")
        m_done, m_hi, m_lo = sem("m_done"), sem("m_hi"), sem("m_lo")
        s2_done, s2_made = sem("s2_done"), sem("s2_made")
        s3_done, s3_hi, s3_lo = sem("s3_done"), sem("s3_hi"), sem("s3_lo")
        z_done = [sem(f"z_done{n}") for n in range(K)]
        y_hi = [sem(f"y_hi{n}") for n in range(2)]
        y_lo = [sem(f"y_lo{n}") for n in range(2)]
        out_made = sem("out_made")

        def rounds(eng, one):
            for i in range(ROUND):
                one(i, i)
            with eng.Fori(1, N_PAIRS // ROUND - 1) as turn:
                for k in range(ROUND):
                    one(turn * ROUND + k, k)
            for i in range(N_PAIRS - ROUND, N_PAIRS + LAG_D):
                one(i, i % ROUND)

        def here(i, lag):
            if isinstance(i, int) and not 0 <= i - lag < N_PAIRS:
                return None
            return i - lag

        def first(i):
            return isinstance(i, int) and i == 0

        def after(i, n):
            return not isinstance(i, int) or i >= n

        def landed(i, k):
            return (i - k) * (16 // ROUND) + 16

        BIAS_LOADS = 1 + G + 2

        block = ctx.enter_context(nc.Block())

        @block.sync
        def _(sp):
            def load_x(i, k):
                if after(i, ROUND):
                    sp.wait_ge(x1_made, i - ROUND + 1)
                sp.dma_start(x_in[k][:], x_pairs(i)).then_inc(x_landed[k], 16)

            def load_adj(i, k):
                if after(i, ROUND):
                    sp.wait_ge(alpha_made, i - ROUND + 1)
                    sp.wait_ge(adjT_done, i - ROUND + 1)
                sp.dma_start(adj_in[k][:], adj_pairs(i)).then_inc(adj_landed[k], 16)

            def x_pairs(i):
                return x[bass.ds(i * G, G)].rearrange("g n d -> n g d")

            def adj_pairs(i):
                return adj[bass.ds(i * G, G)].rearrange("g n m -> n g m")

            def store(i, k):
                sp.wait_ge(out_made, i + 1)
                sp.dma_start(out[bass.ds(i * G, G)].rearrange("g n d -> n g d"),
                             x_out[k][:]).then_inc(stored[k], 16)

            def row(v):
                return v.rearrange("(o d) -> o d", o=1)

            load_x(0, 0)
            sp.dma_start(aw_bc[:], aw.rearrange("(h d) o -> o h d", h=2).to_broadcast([P, 2, D]))\
              .then_inc(score_weights_in, 16)
            sp.dma_start(bv_bc[:], row(bv).to_broadcast([P, D])).then_inc(score_consts_in, 16)
            sp.dma_start(ab_bc[:], row(ab).to_broadcast([P, 1])).then_inc(score_consts_in, 16)
            load_adj(0, 0)
            load_x(1, 1)
            load_adj(1, 1)
            sp.dma_start(bk_bc[:], bk.rearrange("(o k) d -> o k d", o=1).to_broadcast([P, K, D]))\
              .then_inc(biases_in, 16)
            for g in range(G):
                sp.dma_start(bias_out[:, g, :], row(b3).to_broadcast([P, D])).then_inc(biases_in, 16)
            for n, b in enumerate((b1, b2)):
                sp.dma_start(bias_col[n][:], b.rearrange("(c p) -> p c", p=P),
                             allow_slow_non_contiguous=True).then_inc(biases_in, 16)
            for n, w in enumerate((W1, W2, W3)):
                sp.dma_start(w_raw[:, K + n], w.rearrange("(c p) d -> p c d", p=P))\
                  .then_inc(gcn_weights_in[n], 16)

            def one(i, k):
                if (n := here(i, -2)) is not None:
                    load_x(n, (k + 2) % ROUND)
                    load_adj(n, (k + 2) % ROUND)
                if (n := here(i, LAG_D)) is not None:
                    store(n, (k - LAG_D) % ROUND)

            rounds(sp, one)
            for k in range(ROUND):
                sp.wait_ge(stored[k], 16 * (N_PAIRS // ROUND))

        @block.gpsimd
        def _(pool):
            pool.memset(ident[:], 0.0).then_inc(ident_zero, 1)
            pool.memset(minus_half[:], -0.5).then_inc(exponent_made, 1)
            pool.wait_ge(ident_zero, 1)
            pool.affine_select(out=ident[:], in_=ident[:], compare_op=ALU.not_equal, fill=1.0, base=0,
                               pattern=[[-1, P]], channel_multiplier=1).then_inc(ident_made, 1)
            pool.wait_ge(exponent_made, 1)

            def power(n, i, k):
                pool.wait_ge(veps_made[n], i + 1)
                if after(i, 2):
                    pool.wait_ge(norm_made[n], i - 1)
                pool.tensor_tensor(rstd[n][k % 2][:], veps[n][k % 2][:], minus_half[:], ALU.pow)\
                    .then_inc(rstd_made[n], 1)

            def y_low(n, i, k):
                pool.wait_ge(y_hi[n], i + 1)
                if after(i, 1):
                    pool.wait_ge((s2_done, s3_done)[n], i)
                pool.tensor_tensor(y[n][1][:], y_full[n][:], plain(y[n][0][:]), ALU.subtract)\
                    .then_inc(y_lo[n], 1)

            def out_bias(i, k):
                pool.wait_ge(x1_made, i + 1)
                if first(i):
                    pool.wait_ge(biases_in, 16 * BIAS_LOADS)
                if after(i, 4):
                    pool.wait_ge(out_made, i - 3)
                pool.tensor_tensor(x1b[k][:], x1[k % 2][:], bias_out[:], ALU.add).then_inc(x1b_made, 1)

            power(0, 0, 0)

            def sum_biases():
                pool.wait_ge(biases_in, 16 * BIAS_LOADS)
                pool.tensor_tensor(bias_part[:], bk_bc[:, 0, :], bk_bc[:, 1, :], ALU.add)\
                    .then_inc(bias_h_made, 1)
                pool.wait_ge(bias_h_made, 1)
                for g in range(G):
                    pool.tensor_tensor(bias_h[:, g, :], bias_part[:], bk_bc[:, 2, :], ALU.add)\
                        .then_inc(bias_h_made, 1)

            def one(i, k):
                b, c = here(i, LAG_B), here(i, LAG_C)
                if c is not None:
                    y_low(0, c, k - LAG_C)
                if b is not None:
                    power(1, b, k - LAG_B)
                    out_bias(b, (k - LAG_B) % ROUND)
                if (n := here(i, -1)) is not None:
                    power(0, n, k + 1)
                if first(i):
                    sum_biases()
                if c is not None:
                    y_low(1, c, k - LAG_C)

            rounds(pool, one)

        @block.scalar
        def _(act):
            act.dma_start(wv_raw[:], Wv.rearrange("(c p) d -> p c d", p=P)).then_inc(score_weights_in, 16)
            for n, landing in ((2, p2_weights_in), (0, p01_weights_in), (1, p01_weights_in)):
                act.dma_start(w_raw[:, n], Wk[n].rearrange("(c p) d -> p c d", p=P)).then_inc(landing, 16)

            act.wait_ge(p2_weights_in, 16)
            act.activation(w_p2[0][:, :, 0:D], w_raw[:, 2], ACT.Copy).then_inc(k_weights_hi, 1)
            act.wait_ge(p01_weights_in, 16 * 2)
            for n in range(2):
                act.activation(w_p01[0][:, :, n * D:(n + 1) * D], w_raw[:, n], ACT.Copy)\
                   .then_inc(k_weights_hi, 1)

            def hT_high(i, k):
                act.wait_ge(hT_done, i + 1)
                if after(i, 2):
                    act.wait_ge(p01_done, i - 1)
                act.activation(h0T[k % 2][0][:], turned_ps, ACT.Relu).then_inc(hT_hi, 1)

            def adjT_high(i, k):
                act.wait_ge(adjT_done, i + 1)
                if after(i, 4):
                    act.wait_ge(z_done[2], i - 3)
                act.activation(adjT_full[k][:], T_ps, ACT.Copy)
                act.activation(adjT[k][0][:], T_ps, ACT.Copy).then_inc(adjT_hi, 1)

            def scores_copy(i, k):
                act.wait_ge(p2_done, i + 1)
                if first(i):
                    act.wait_ge(half_c_made, 1)
                if after(i, 2):
                    act.wait_ge(spread_done, i - 1)
                    act.wait_ge(z_made, i - 1)
                act.activation(uv[k % 2][:], uv_ps, ACT.Identity, bias=half_c[:]).then_inc(uv_made, 1)

            def p2_high(i, k):
                if after(i, 2):
                    act.wait_ge(y1_done, i - 1)
                act.activation(p2[k % 2][0][:], p2_ps, ACT.Copy).then_inc(p2_hi, 1)

            def logits(i, k):
                act.wait_ge(spread_done, i + 1)
                act.wait_ge(uv_made, i + 1)
                if after(i, 2):
                    act.wait_ge(exp_made, i - 1)
                act.activation(z[k % 2][:, 0, :], T_ps[:, 0, :], ACT.Identity, bias=uv[k % 2][:, 0, 1:2])
                act.activation(z[k % 2][:, 1, :], T_ps[:, 1, :], ACT.Identity, bias=uv[k % 2][:, 1, 1:2])\
                   .then_inc(z_made, 1)

            def exponentials(i, k):
                act.wait_ge(leaky_made, i + 1)
                if after(i, 2):
                    act.wait_ge(alpha_made, i - 1)
                act.activation(e[k % 2][:], z[k % 2][:], ACT.Exp).then_inc(exp_made, 1)

            def tT_high(i, k):
                act.wait_ge(tT_done, i + 1)
                if after(i, 2):
                    act.wait_ge(h_done, i - 1)
                act.activation(tT[k % 2][0][:], T_ps, ACT.Copy).then_inc(tT_hi, 1)

            def y1_high(i, k):
                act.wait_ge(y1_done, i + 1)
                if after(i, 2):
                    act.wait_ge(h_done, i - 1)
                act.activation(y1[k % 2][0][:], p1_ps, ACT.Copy).then_inc(y1_hi, 1)

            def norm(i, k):
                act.wait_ge(shift_made, i + 1)
                if after(i, 2):
                    act.wait_ge(m_done, i - 1)
                for g in range(G):
                    last = act.activation(h1[k % 2][:, g, :], x1[k % 2][:, g, :], ACT.Relu,
                                          bias=nshift[k % 2][:, g:g + 1], scale=rstd[1][k % 2][:, g:g + 1])
                last.then_inc(norm_made[1], 1)

            def m_high(i):
                act.wait_ge(m_done, i + 1)
                if after(i, 1):
                    act.wait_ge(z_done[0], i)
                act.activation(m[0][:], turned_ps, ACT.Copy).then_inc(m_hi, 1)

            def s2_copy(i):
                act.wait_ge(s2_done, i + 1)
                if after(i, 1):
                    act.wait_ge(z_done[1], i)
                act.activation(s2[:], s2_ps, ACT.Copy).then_inc(s2_made, 1)

            def s3_high(i):
                act.wait_ge(s3_done, i + 1)
                if after(i, 1):
                    act.wait_ge(z_done[2], i)
                act.activation(s3[0][:], s3_ps, ACT.Copy).then_inc(s3_hi, 1)

            def y_full_copy(n, i):
                act.wait_ge(z_done[n], i + 1)
                if first(i):
                    act.wait_ge(biases_in, 16 * BIAS_LOADS)
                if after(i, 1):
                    act.wait_ge(y_lo[n], i)
                for c in range(C):
                    act.activation(y_full[n][:, c], (z1_ps, z2_ps)[n][:, c], ACT.Relu,
                                   bias=bias_col[n][:, c:c + 1])

            def y_high(n, i):
                if after(i, 1):
                    act.wait_ge((s2_done, s3_done)[n], i)
                for c in range(C):
                    last = act.activation(y[n][0][:, c], (z1_ps, z2_ps)[n][:, c], ACT.Relu,
                                          bias=bias_col[n][:, c:c + 1])
                last.then_inc(y_hi[n], 1)

            def one(i, k):
                a, b, c = here(i, 0), here(i, LAG_B), here(i, LAG_C)
                kb = (k - LAG_B) % ROUND
                if a is not None:
                    hT_high(a, k)
                if c is not None:
                    y_full_copy(0, c)
                    y_high(0, c)
                if a is not None:
                    adjT_high(a, k)
                    scores_copy(a, k)
                    p2_high(a, k)
                if c is not None:
                    s2_copy(c)
                if a is not None:
                    logits(a, k)
                if b is not None:
                    norm(b, kb)
                if a is not None:
                    exponentials(a, k)
                if first(i):
                    for n in range(K):
                        act.wait_ge(gcn_weights_in[n], 16)
                        act.activation(w_gcn[n][0][:], w_raw[:, K + n], ACT.Copy).then_inc(gcn_weights_hi, 1)
                if c is not None:
                    y_full_copy(1, c)
                    y_high(1, c)
                if b is not None:
                    m_high(b)
                if a is not None:
                    tT_high(a, k)
                if c is not None:
                    s3_high(c)
                if a is not None:
                    y1_high(a, k)

            rounds(act, one)


        @block.vector
        def _(dve):
            def low(dst, src, hi, signal):
                dve.tensor_tensor(dst, src, plain(hi), ALU.subtract).then_inc(signal, 1)

            def statistics(n, i, k, src):
                if after(i, 2):
                    dve.wait_ge(mv_made[n], i - 1)
                for g in range(G):
                    last = dve.bn_stats(stats[n][k % 2][:, g, :], src[:, g, :])
                last.then_inc(stats_made[n], 1)

            def moments(n, i, k, between):
                dve.wait_ge(stats_made[n], i + 1)
                if after(i, 2):
                    dve.wait_ge((norm_made[0], shift_made)[n], i - 1)
                between()
                for g in range(G):
                    last = dve.bn_aggr(mv[n][k % 2][:, g, :], stats[n][k % 2][:, g, :])
                last.then_inc(mv_made[n], 1)

            def guard_variance(n, i, k):
                dve.wait_ge(mv_made[n], i + 1)
                if after(i, 2):
                    dve.wait_ge(rstd_made[n], i - 1)
                dve.tensor_scalar(veps[n][k % 2][:], mv[n][k % 2][:, :, 1], LN_EPS, None, ALU.add)\
                   .then_inc(veps_made[n], 1)

            def x_statistics(i, k):
                dve.wait_ge(x_landed[k], landed(i, k))
                statistics(0, i, k, x_in[k])

            def x_norm(i, k):
                dve.wait_ge(rstd_made[0], i + 1)
                if after(i, 2):
                    dve.wait_ge(hT_done, i - 1)
                for g in range(G):
                    last = dve.tensor_scalar(n0[k % 2][:, g, :], x_in[k][:, g, :], mv[0][k % 2][:, g, 0:1],
                                             rstd[0][k % 2][:, g:g + 1], ALU.subtract, ALU.mult)
                last.then_inc(norm_made[0], 1)

            def shift(i, k):
                dve.wait_ge(rstd_made[1], i + 1)
                if after(i, 2):
                    dve.wait_ge(norm_made[1], i - 1)
                dve.scalar_tensor_tensor(nshift[k % 2][:], mv[1][k % 2][:, :, 0], -1.0, rstd[1][k % 2][:],
                                         ALU.mult, ALU.mult).then_inc(shift_made, 1)

            def hT_low(i, k):
                hi, lo = h0T[k % 2]
                dve.wait_ge(hT_hi, i + 1)
                if after(i, 2):
                    dve.wait_ge(p01_done, i - 1)
                dve.scalar_tensor_tensor(lo[:], turned_ps, 0.0, plain(hi[:]), ALU.max, ALU.subtract)\
                   .then_inc(hT_lo, 1)

            def adjT_low(i, k):
                dve.wait_ge(adjT_hi, i + 1)
                if after(i, 4):
                    dve.wait_ge(z_done[2], i - 3)
                low(adjT[k][1][:], T_ps, adjT[k][0][:], adjT_lo)

            def p2_low(i, k):
                dve.wait_ge(p2_hi, i + 1)
                if after(i, 2):
                    dve.wait_ge(y1_done, i - 1)
                low(p2[k % 2][1][:], p2_ps, p2[k % 2][0][:], p2_lo)

            def leaky(i, k):
                dve.wait_ge(z_made, i + 1)
                zz = z[k % 2][:]
                dve.scalar_tensor_tensor(zz, zz, SLOPE, zz, ALU.mult, ALU.max).then_inc(leaky_made, 1)

            def attention(i, k):
                dve.wait_ge(exp_made, i + 1)
                dve.wait_ge(adj_landed[k], landed(i, k))
                if after(i, 2):
                    dve.wait_ge(tn_made, i - 1)
                for g in range(G):
                    last = dve.tensor_tensor_reduce(alpha[k % 2][:, g, :], adj_in[k][:, g, :],
                                                    e[k % 2][:, g, :], 1.0, 0.0, ALU.mult, ALU.add,
                                                    rowsum[k % 2][:, g:g + 1])
                last.then_inc(alpha_made, 1)

            def guard_sum(i, k):
                dve.wait_ge(alpha_made, i + 1)
                dve.tensor_scalar(rowsum[k % 2][:], rowsum[k % 2][:], DIV_EPS, None, ALU.add)\
                   .then_inc(sum_guarded, 1)

            def invert_sum(i, k):
                dve.wait_ge(sum_guarded, i + 1)
                dve.reciprocal(rinv[k % 2][:], rowsum[k % 2][:]).then_inc(rinv_made, 1)

            def transition(i, k):
                dve.wait_ge(rinv_made, i + 1)
                if after(i, 2):
                    dve.wait_ge(tT_done, i - 1)
                for g in range(G):
                    last = dve.tensor_scalar(tn[k % 2][:, g, :], alpha[k % 2][:, g, :],
                                             rinv[k % 2][:, g:g + 1], None, ALU.mult)
                last.then_inc(tn_made, 1)

            def tT_low(i, k):
                dve.wait_ge(tT_hi, i + 1)
                if after(i, 2):
                    dve.wait_ge(h_done, i - 1)
                low(tT[k % 2][1][:], T_ps, tT[k % 2][0][:], tT_lo)

            def y1_low(i, k):
                dve.wait_ge(y1_hi, i + 1)
                if after(i, 2):
                    dve.wait_ge(h_done, i - 1)
                low(y1[k % 2][1][:], p1_ps, y1[k % 2][0][:], y1_lo)

            def h_bias(i, k):
                dve.wait_ge(h_done, i + 1)
                if first(i):
                    dve.wait_ge(bias_h_made, 1 + G)
                if after(i, 2):
                    dve.wait_ge(x1_made, i - 1)
                dve.tensor_tensor(hb[k % 2][:], p0_ps, bias_h[:], ALU.add).then_inc(hb_made, 1)

            def residual(i, k):
                dve.wait_ge(hb_made, i + 1)
                if after(i, 2):
                    dve.wait_ge(x1b_made, i - 1)
                    dve.wait_ge(norm_made[1], i - 1)
                dve.scalar_tensor_tensor(x1[k % 2][:], hb[k % 2][:], 0.0, x_in[k][:], ALU.max, ALU.add)\
                   .then_inc(x1_made, 1)

            def x1_statistics(i, k):
                dve.wait_ge(x1_made, i + 1)
                statistics(1, i, k, x1[k % 2])

            def m_low(i):
                dve.wait_ge(m_hi, i + 1)
                if after(i, 1):
                    dve.wait_ge(z_done[0], i)
                low(m[1][:], turned_ps, m[0][:], m_lo)

            def s3_low(i):
                dve.wait_ge(s3_hi, i + 1)
                if after(i, 1):
                    dve.wait_ge(z_done[2], i)
                low(s3[1][:], s3_ps, s3[0][:], s3_lo)

            def finish(i, k):
                dve.wait_ge(z_done[2], i + 1)
                dve.wait_ge(x1b_made, i + 1)
                if after(i, 4):
                    dve.wait_ge(stored[k], landed(i - ROUND, k))
                dve.tensor_tensor(x_out[k][:], z3_ps, x1b[k][:], ALU.add).then_inc(out_made, 1)

            x_statistics(0, 0)
            moments(0, 0, 0, lambda: None)
            guard_variance(0, 0, 0)
            dve.wait_ge(score_weights_in, 16 * 2)
            dve.wait_ge(score_consts_in, 16 * 2)
            for h in range(2):
                dve.tensor_tensor_reduce(scratch[:, 4 + h, :], bv_bc[:], aw_bc[:, h, :],
                                         1.0, 0.0, ALU.mult, ALU.add, bva[:, h:h + 1]).then_inc(bva_made, 1)
            for c in range(C):
                for h in range(2):
                    dve.tensor_tensor_reduce(scratch[:, 2 * c + h, :], wv_raw[:, c, :], aw_bc[:, h, :],
                                             1.0, 0.0, ALU.mult, ALU.add, wva[:, c, h:h + 1])\
                       .then_inc(wva_made, 1)
            dve.wait_ge(bva_made, 2)
            dve.tensor_tensor(c_sum[:, 0:1], bva[:, 0:1], bva[:, 1:2], ALU.add).then_inc(c_summed, 1)
            x_norm(0, 0)
            dve.wait_ge(c_summed, 1)
            dve.tensor_tensor(c_sum[:, 1:2], c_sum[:, 0:1], ab_bc[:], ALU.add).then_inc(c_summed, 1)
            dve.wait_ge(wva_made, 2 * C)
            dve.tensor_copy(w_p2[0][:, :, D:D + 2], wva[:]).then_inc(p2_weights_cut, 1)
            dve.wait_ge(k_weights_hi, 1)
            low(w_p2[1][:, :, 0:D], w_raw[:, 2], w_p2[0][:, :, 0:D], p2_weights_cut)
            dve.wait_ge(p2_weights_cut, 1)
            low(w_p2[1][:, :, D:D + 2], wva[:], w_p2[0][:, :, D:D + 2], p2_weights_cut)
            dve.wait_ge(c_summed, 2)
            dve.tensor_scalar(half_c[:], c_sum[:, 1:2], 0.5, None, ALU.mult).then_inc(half_c_made, 1)
            for n in range(2):
                dve.wait_ge(k_weights_hi, 2 + n)
                cols = slice(n * D, (n + 1) * D)
                low(w_p01[1][:, :, cols], w_raw[:, n], w_p01[0][:, :, cols], p01_weights_cut)

            def one(i, k):
                a, b, c, d = here(i, 0), here(i, LAG_B), here(i, LAG_C), here(i, LAG_D)
                nxt = here(i, -1)
                kb, kd, kn = (k - LAG_B) % ROUND, (k - LAG_D) % ROUND, (k + 1) % ROUND
                if a is not None:
                    hT_low(a, k)
                if b is not None:
                    h_bias(b, kb)
                    residual(b, kb)
                    x1_statistics(b, kb)
                    moments(1, b, kb, lambda: adjT_low(a, k) if a is not None else None)
                    guard_variance(1, b, kb)
                elif a is not None:
                    adjT_low(a, k)
                if a is not None:
                    p2_low(a, k)
                if b is not None:
                    shift(b, kb)
                if a is not None:
                    leaky(a, k)
                if nxt is not None:
                    x_statistics(nxt, kn)
                if d is not None:
                    finish(d, kd)
                if nxt is not None:
                    moments(0, nxt, kn, lambda: attention(a, k))
                    guard_variance(0, nxt, kn)
                elif a is not None:
                    attention(a, k)
                if a is not None:
                    guard_sum(a, k)
                    invert_sum(a, k)
                    transition(a, k)
                if nxt is not None:
                    x_norm(nxt, kn)
                if first(i):
                    for n in range(K):
                        dve.wait_ge(gcn_weights_hi, n + 1)
                        low(w_gcn[n][1][:], w_raw[:, K + n], w_gcn[n][0][:], gcn_weights_cut)
                if b is not None:
                    m_low(b)
                if a is not None:
                    tT_low(a, k)
                if c is not None:
                    s3_low(c)
                if a is not None:
                    y1_low(a, k)

            rounds(dve, one)

        @block.tensor
        def _(pe):
            HI, LO = 0, 1
            PARTS = ((HI, HI), (HI, LO), (LO, HI))

            def matmul(dst, stationary, moving, start, stop):
                return pe.matmul(dst, stationary, moving, start=start, stop=stop, skip_group_check=True)

            def turn_h(i, k):
                pe.wait_ge(norm_made[0], i + 1)
                if after(i, 2):
                    pe.wait_ge(m_lo, i - 1)
                elif not first(i):
                    pe.wait_ge(hT_lo, i)
                for c in range(C):
                    for g in range(G):
                        last = pe.transpose(turned_ps[:, c, g, :], n0[k % 2][:, g, c * P:(c + 1) * P],
                                            ident[:])
                last.then_inc(hT_done, 1)

            def turn_adj(i, k):
                pe.wait_ge(adj_landed[k], landed(i, k))
                if after(i, 1):
                    pe.wait_ge(tT_lo, i)
                for g in range(G):
                    last = pe.transpose(T_ps[:, g, :], adj_in[k][:, g, :], ident[:])
                last.then_inc(adjT_done, 1)

            def spread_scores(i, k):
                pe.wait_ge(uv_made, i + 1)
                pe.wait_ge(adjT_lo, i + 1)
                for g in range(G):
                    last = pe.transpose(T_ps[:, g, :], uv[k % 2][:, g, 0:1].to_broadcast([P, P]), ident[:])
                last.then_inc(spread_done, 1)

            def turn_T(i, k):
                pe.wait_ge(tn_made, i + 1)
                pe.wait_ge(z_made, i + 1)
                for g in range(G):
                    last = pe.transpose(T_ps[:, g, :], tn[k % 2][:, g, :], ident[:])
                last.then_inc(tT_done, 1)

            def times_weights(hT, w, dst, starts, lo_wait):
                steps = [(g, c, a, b) for low in (False, True) for g in range(G) for c in range(C)
                         for a, b in PARTS if (a == LO) == low]
                for n, (g, c, a, b) in enumerate(steps):
                    if a == LO and steps[n - 1][2] == HI:
                        lo_wait()
                    start = c == 0 and a == HI and b == HI and g in starts
                    last = matmul(dst[g], hT[a][:, c, g, :], w[b][:, c, :], start, a == LO and c == C - 1)
                return last

            def p2_product(i, k):
                pe.wait_ge(hT_hi, i + 1)
                if first(i):
                    pe.wait_ge(p2_weights_cut, 3)
                if after(i, 1):
                    pe.wait_ge(p2_lo, i)
                times_weights(h0T[k % 2], w_p2, [bank_p2[:, g, 0:D + 2] for g in range(G)], range(G),
                              lambda: pe.wait_ge(hT_lo, i + 1)).then_inc(p2_done, 1)

            def p01_product(i, k, g):
                if g == 0 and first(i):
                    pe.wait_ge(p01_weights_cut, 2)
                if g == 0 and after(i, 1):
                    pe.wait_ge(hb_made, i)
                for c in range(C):
                    for a, b in PARTS:
                        last = matmul(bank_p[:, g, :], h0T[k % 2][a][:, c, g, :], w_p01[b][:, c, :],
                                      c == 0 and (a, b) == (HI, HI), c == C - 1 and a == LO)
                if g == G - 1:
                    last.then_inc(p01_done, 1)

            def times_T(dst, t, src, g, a, b):
                return matmul(dst[:, g, :], t[a][:, g, :], src[b][:, g, :], False, (a, b) == (LO, HI))

            def y1_product(i, k):
                pe.wait_ge(tT_hi, i + 1)
                pe.wait_ge(p2_lo, i + 1)
                for g in range(G):
                    for a, b in ((HI, HI), (HI, LO)):
                        times_T(p1_ps, tT[k % 2], p2[k % 2], g, a, b)
                pe.wait_ge(tT_lo, i + 1)
                for g in range(G):
                    last = times_T(p1_ps, tT[k % 2], p2[k % 2], g, LO, HI)
                last.then_inc(y1_done, 1)

            def h_product(i, k):
                pe.wait_ge(y1_lo, i + 1)
                for g in range(G):
                    for a, b in PARTS:
                        last = times_T(p0_ps, tT[k % 2], y1[k % 2], g, a, b)
                last.then_inc(h_done, 1)

            def aggregate(dst, src, i, k):
                for g in range(G):
                    for c in range(C):
                        last = matmul(dst[:, c, g, :], src[:, g, c * P:(c + 1) * P],
                                      adjT_full[k][:, g, :], g == 0 and c == 0, True)
                return last

            def m_product(i, k):
                pe.wait_ge(norm_made[1], i + 1)
                pe.wait_ge(adjT_hi, i + 1)
                if here(i, -LAG_B) is not None:
                    pe.wait_ge(hT_lo, i + LAG_B + 1)
                else:
                    pe.wait_ge(m_lo, i)
                aggregate(turned_ps, h1[k % 2], i, k).then_inc(m_done, 1)

            def z1_product(i):
                pe.wait_ge(m_hi, i + 1)
                if first(i):
                    pe.wait_ge(gcn_weights_cut, K)
                if after(i, 1):
                    pe.wait_ge(y_hi[1], i)
                steps = [(o, c, a, b) for low in (False, True) for o in range(C) for c in range(C)
                         for b, a in PARTS if (b == LO) == low]
                for n, (o, c, a, b) in enumerate(steps):
                    if b == LO and steps[n - 1][3] == HI:
                        pe.wait_ge(m_lo, i + 1)
                    last = matmul(z1_ps[:, o], w_gcn[0][a][:, c, o * P:(o + 1) * P], m[b][:, c],
                                  n == 0, b == LO and c == C - 1)
                last.then_inc(z_done[0], 1)

            def s2_product(i):
                pe.wait_ge(y_hi[0], i + 1)
                times_weights(y[0], w_gcn[1], [s2_ps[:, g, :] for g in range(G)], (0,),
                              lambda: pe.wait_ge(y_lo[0], i + 1)).then_inc(s2_done, 1)

            def z2_product(i, k):
                pe.wait_ge(s2_made, i + 1)
                aggregate(z2_ps, s2, i, k).then_inc(z_done[1], 1)

            def s3_product(i):
                pe.wait_ge(y_hi[1], i + 1)
                if after(i, 1):
                    pe.wait_ge(out_made, i)
                times_weights(y[1], w_gcn[2], [s3_ps[:, g, :] for g in range(G)], (0,),
                              lambda: pe.wait_ge(y_lo[1], i + 1)).then_inc(s3_done, 1)

            def z3_product(i, k):
                pe.wait_ge(s3_lo, i + 1)
                pe.wait_ge(adjT_lo, i + 1)
                for g in range(G):
                    for a, b in PARTS:
                        last = matmul(z3_ps[:, g, :], adjT[k][a][:, g, :], s3[b][:, g, :],
                                      g == 0 and (a, b) == (HI, HI), (a, b) == (LO, HI))
                last.then_inc(z_done[2], 1)

            pe.wait_ge(ident_made, 1)

            def one(i, k):
                a, b, c, d = here(i, 0), here(i, LAG_B), here(i, LAG_C), here(i, LAG_D)
                kb, kc, kd = (k - LAG_B) % ROUND, (k - LAG_C) % ROUND, (k - LAG_D) % ROUND
                if a is not None:
                    turn_h(a, k)
                    turn_adj(a, k)
                if b is not None:
                    h_product(b, kb)
                if a is not None:
                    p2_product(a, k)
                if d is not None:
                    z3_product(d, kd)
                if c is not None:
                    s2_product(c)
                if a is not None:
                    spread_scores(a, k)
                    p01_product(a, k, 0)
                if c is not None:
                    z2_product(c, kc)
                if a is not None:
                    p01_product(a, k, 1)
                if b is not None:
                    m_product(b, kb)
                if a is not None:
                    turn_T(a, k)
                if c is not None:
                    s3_product(c)
                if a is not None:
                    y1_product(a, k)
                if b is not None:
                    z1_product(b)

            rounds(pe, one)


_OUT = "x_new"


def kernel(**inputs):
    import numpy as np
    import concourse.bacc as bacc
    from concourse.bass_utils import run_bass_kernel_spmd

    nc = bacc.Bacc("TRN2", target_bir_lowering=False, num_devices=1)
    arrays, args = {}, []
    for name in ("x", "adj", *("L0_gnn_" + n for n in ("Wv", "bv", "aw", "ab", "Wk", "bk")),
                 *("L1_gnn_" + n for n in ("W1", "b1", "W2", "b2", "W3", "b3"))):
        a = np.ascontiguousarray(inputs[name])
        arrays["in_" + name] = a
        args.append(nc.dram_tensor("in_" + name, a.shape, mybir.dt.from_np(a.dtype), kind="ExternalInput").ap())
    args.append(nc.dram_tensor(_OUT, inputs["x"].shape, F32, kind="ExternalOutput").ap())
    gnn_kernel(nc, *args)
    return run_bass_kernel_spmd(nc, [arrays], core_ids=[0]).results[0][_OUT]
```

```python
from contextlib import ExitStack

import concourse.bass as bass
import concourse.mybir as mybir

F32 = mybir.dt.float32
F32R = mybir.dt.float32r
ALU = mybir.AluOpType
ACT = mybir.ActivationFunctionType

P = 128
SQUARE = 32
G = 2
C = 2
D = C * P
K = 3
BUSY_BEFORE, BUSY_BETWEEN, BUSY_SECOND, BUSY_TAIL = 19, 18, 19, 16
ROUND = 4
BODY = 2 * ROUND
LAG_B, LAG_C, LAG_D = 1, 2, 3
LN_EPS = 1e-5
DIV_EPS = 1e-12
HEADROOM = 2.0 ** -16
SLOPE = 0.2


def gnn_kernel(nc, x, adj, Wv, bv, aw, ab, Wk, bk, W1, b1, W2, b2, W3, b3, out):
    N_PAIRS = x.shape[0] // G
    ctx = ExitStack()
    with ctx:
        def sb(name, shape, dt=F32):
            return ctx.enter_context(nc.sbuf_tensor(name, shape, dt))

        def sem(name):
            return ctx.enter_context(nc.semaphore(name))

        def hilo(name, shape):
            return [sb(name + "_hi", shape, F32R), sb(name + "_lo", shape, F32R)]

        def plain(ap):
            return ap.bitcast(F32)

        ident = sb("ident", [P, P])
        w_raw = sb("w_raw", [P, 2 * K, C, D])
        wv_raw = sb("wv_raw", [P, C, D])
        w_p2 = hilo("w_p2", [P, C, D + 2])
        w_p01 = hilo("w_p01", [P, C, 2 * D])
        w_gcn = [hilo(f"w_gcn{n}", [P, C, D]) for n in range(K)]
        wva = sb("wva", [P, C, 2])
        aw_bc = sb("aw_bc", [P, 2, D])
        bv_bc = sb("bv_bc", [P, D])
        ab_bc = sb("ab_bc", [P, 1])
        bk_bc = sb("bk_bc", [P, K, D])
        scratch = sb("scratch", [P, 6, D])
        bva = sb("bva", [P, 2])
        half_c = sb("half_c", [P, 1])
        c_sum = sb("c_sum", [P, 2])
        bias_h = sb("bias_h", [P, G, D])
        bias_part = sb("bias_part", [P, D])
        bias_out = sb("bias_out", [P, G, D])
        bias_col = [sb(f"bias_col{n}", [P, C]) for n in range(2)]
        minus_half = sb("minus_half", [P, G])

        def slots(n, name, shape, dt=F32):
            return [sb(f"{name}{s}", shape, dt) for s in range(n)]

        def slots_hilo(n, name, shape):
            return [hilo(f"{name}{s}", shape) for s in range(n)]

        x_in = slots(4, "x_in", [P, G, D])
        adj_blocks = slots(4, "adj_blocks", [P, G, P])
        adjT_full = slots(4, "adjT_full", [P, G, P])
        adjT = slots_hilo(4, "adjT", [P, G, P])
        x1b = slots(4, "x1b", [P, G, D])
        x_out = slots(4, "x_out", [P, G, D])
        stats = [slots(2, f"stats{n}_", [P, G, 6]) for n in range(2)]
        mv = [slots(2, f"mv{n}_", [P, G, 2]) for n in range(2)]
        veps = [slots(2, f"veps{n}_", [P, G]) for n in range(2)]
        rstd = [slots(2, f"rstd{n}_", [P, G]) for n in range(2)]
        nshift = slots(2, "nshift", [P, G])
        n0 = slots(2, "n0_", [P, G, D])
        h1 = slots(2, "h1_", [P, G, D])
        h0T = slots_hilo(2, "h0T", [P, C, G, P])
        uv = slots(2, "uv", [P, G, 2])
        z = slots(2, "z", [P, G, P])
        e = slots(2, "e", [P, G, P])
        alpha = slots(2, "alpha", [P, G, P])
        aT = slots_hilo(2, "aT", [P, G, P])
        sums = slots(2, "sums", [P, G])
        rinv = slots(2, "rinv", [P, G])
        p2 = slots_hilo(2, "p2_", [P, G, D + 2])
        y1_full = slots(2, "y1_full", [P, G, D])
        y1 = slots_hilo(2, "y1_", [P, G, D])
        p0b = slots(2, "p0b", [P, G, D])
        p1 = slots(2, "p1_", [P, G, D])
        hb = slots(2, "hb", [P, G, D])
        x1 = slots(2, "x1_", [P, G, D])
        m = hilo("m", [P, C, G, P])
        s2 = sb("s2", [P, G, D])
        s3 = hilo("s3", [P, G, D])
        y_full = [sb(f"y_full{n}", [P, C, G, P]) for n in range(2)]
        y = [hilo(f"y{n}_", [P, C, G, P]) for n in range(2)]

        def bank(name):
            return ctx.enter_context(nc.psum_tensor(name, [P, 512], F32))

        bank_turned = bank("bank_turned")
        bank_T = bank("bank_T")
        bank_p = ctx.enter_context(nc.psum_tensor("bank_p", [P, G, 512], F32))
        bank_p2 = ctx.enter_context(nc.psum_tensor("bank_p2", [P, G, 512], F32))
        bank_2 = bank("bank_2")
        bank_3 = bank("bank_3")
        turned_ps = bank_turned[:].rearrange("p (c g n) -> p c g n", c=C, g=G)
        spread_ps = bank_T[:, 0:G * P].rearrange("p (g n) -> p g n", g=G)
        ay_ps = bank_T[:].rearrange("p (g d) -> p g d", g=G)
        p0_ps = bank_p[:, :, 0:D]
        p1_ps = bank_p[:, :, D:2 * D]
        p2_ps = bank_p2[:, :, 0:D]
        uv_ps = bank_p2[:, :, D:D + 2]
        sums_ps = bank_p2[:, :, D]
        z1_ps = bank_2[:].rearrange("p (c g n) -> p c g n", c=C, g=G)
        s2_ps = bank_2[:].rearrange("p (g d) -> p g d", g=G)
        z2_ps = bank_2[:].rearrange("p (c g n) -> p c g n", c=C, g=G)
        s3_ps = bank_3[:].rearrange("p (g d) -> p g d", g=G)
        z3_ps = bank_3[:].rearrange("p (g d) -> p g d", g=G)

        score_weights_in = sem("score_weights_in")
        score_consts_in = sem("score_consts_in")
        biases_in = sem("biases_in")
        p2_weights_in = sem("p2_weights_in")
        p01_weights_in = sem("p01_weights_in")
        gcn_weights_in = [sem(f"gcn_weights_in{n}") for n in range(K)]
        ident_zero, ident_made = sem("ident_zero"), sem("ident_made")
        exponent_made = sem("exponent_made")
        half_c_made = sem("half_c_made")
        wva_made, bva_made, c_summed = sem("wva_made"), sem("bva_made"), sem("c_summed")
        bias_h_made = sem("bias_h_made")
        k_weights_hi = sem("k_weights_hi")
        score_columns_hi = sem("score_columns_hi")
        p2_weights_cut = sem("p2_weights_cut")
        p01_weights_cut = sem("p01_weights_cut")
        gcn_weights_hi = sem("gcn_weights_hi")
        gcn_weights_cut = sem("gcn_weights_cut")
        x_landed = [sem(f"x_landed{k}") for k in range(ROUND)]
        blocks_landed = [sem(f"blocks_landed{k}") for k in range(ROUND)]
        stored = [sem(f"stored{k}") for k in range(ROUND)]
        stats_made = [sem(f"stats_made{n}") for n in range(2)]
        mv_made = [sem(f"mv_made{n}") for n in range(2)]
        veps_made = [sem(f"veps_made{n}") for n in range(2)]
        rstd_made = [sem(f"rstd_made{n}") for n in range(2)]
        shift_made = sem("shift_made")
        norm_made = [sem(f"norm_made{n}") for n in range(2)]
        hT_done, hT_hi, hT_lo = sem("hT_done"), sem("hT_hi"), sem("hT_lo")
        adj_turned, adjT_hi, adjT_lo = sem("adj_turned"), sem("adjT_hi"), sem("adjT_lo")
        p01_done = sem("p01_done")
        p2_done, p2_hi, p2_lo = sem("p2_done"), sem("p2_hi"), sem("p2_lo")
        uv_made = sem("uv_made")
        spread_done = sem("spread_done")
        z_made = sem("z_made")
        leaky_made = sem("leaky_made")
        exp_made = sem("exp_made")
        alpha_made = sem("alpha_made")
        aT_hi, aT_lo = sem("aT_hi"), sem("aT_lo")
        ones_made = sem("ones_made")
        ap_done = sem("ap_done")
        sum_guarded = sem("sum_guarded")
        rinv_made = sem("rinv_made")
        y1_made, y1_hi, y1_lo = sem("y1_made"), sem("y1_hi"), sem("y1_lo")
        p0b_made, p1_made = sem("p0b_made"), sem("p1_made")
        ay_done = sem("ay_done")
        h_made = sem("h_made")
        x1_made = sem("x1_made")
        x1b_made = sem("x1b_made")
        m_done, m_hi, m_lo = sem("m_done"), sem("m_hi"), sem("m_lo")
        s2_done, s2_made = sem("s2_done"), sem("s2_made")
        s3_done, s3_hi, s3_lo = sem("s3_done"), sem("s3_hi"), sem("s3_lo")
        z_done = [sem(f"z_done{n}") for n in range(K)]
        y_hi = [sem(f"y_hi{n}") for n in range(2)]
        y_made = [sem(f"y_made{n}") for n in range(2)]
        y_lo = [sem(f"y_lo{n}") for n in range(2)]
        out_made = sem("out_made")

        def rounds(eng, one):
            for i in range(ROUND):
                one(i, i)
            with eng.Fori(0, N_PAIRS // BODY - 1) as turn:
                for k in range(BODY):
                    one(turn * BODY + (ROUND + k), k % ROUND)
            for i in range(N_PAIRS - ROUND, N_PAIRS + LAG_D):
                one(i, i % ROUND)

        def here(i, lag):
            if isinstance(i, int) and not 0 <= i - lag < N_PAIRS:
                return None
            return i - lag

        def first(i):
            return isinstance(i, int) and i == 0

        def second(i):
            return isinstance(i, int) and i == 1

        def tail(i):
            return isinstance(i, int) and i >= N_PAIRS

        def after(i, n):
            return not isinstance(i, int) or i >= n

        def landed(i, k):
            return (i - k) * (16 // ROUND) + 16

        BIAS_LOADS = 1 + G + 2

        block = ctx.enter_context(nc.Block())

        @block.sync
        def _(sp):
            def load_x(i, k):
                if after(i, ROUND):
                    sp.wait_ge(x1_made, i - ROUND + 1)
                sp.dma_start(x_in[k][:], x_pairs(i)).then_inc(x_landed[k], 16)

            def load_adj_blocks(i, k):
                if after(i, ROUND):
                    sp.wait_ge(adj_turned, i - ROUND + 1)
                pair = adj[bass.ds(i * G, G)].rearrange("g (j r) (i s) -> i r g j s", r=SQUARE, s=SQUARE)
                for b in range(P // SQUARE):
                    rows = slice(b * SQUARE, (b + 1) * SQUARE)
                    sp.dma_start(adj_blocks[k][rows].rearrange("r g (j s) -> r g j s", s=SQUARE),
                                 pair[b]).then_inc(blocks_landed[k], 16)

            def x_pairs(i):
                return x[bass.ds(i * G, G)].rearrange("g n d -> n g d")

            def store(i, k):
                sp.wait_ge(out_made, i + 1)
                sp.dma_start(out[bass.ds(i * G, G)].rearrange("g n d -> n g d"),
                             x_out[k][:]).then_inc(stored[k], 16)

            def row(v):
                return v.rearrange("(o d) -> o d", o=1)

            load_x(0, 0)
            sp.dma_start(aw_bc[:], aw.rearrange("(h d) o -> o h d", h=2).to_broadcast([P, 2, D]))\
              .then_inc(score_weights_in, 16)
            sp.dma_start(bv_bc[:], row(bv).to_broadcast([P, D])).then_inc(score_consts_in, 16)
            sp.dma_start(ab_bc[:], row(ab).to_broadcast([P, 1])).then_inc(score_consts_in, 16)
            load_x(1, 1)
            load_adj_blocks(0, 0)
            sp.dma_start(w_raw[:, K], W1.rearrange("(c p) d -> p c d", p=P)).then_inc(gcn_weights_in[0], 16)
            sp.dma_start(bk_bc[:], bk.rearrange("(o k) d -> o k d", o=1).to_broadcast([P, K, D]))\
              .then_inc(biases_in, 16)
            load_adj_blocks(1, 1)
            for g in range(G):
                sp.dma_start(bias_out[:, g, :], row(b3).to_broadcast([P, D])).then_inc(biases_in, 16)
            for n, b in enumerate((b1, b2)):
                sp.dma_start(bias_col[n][:], b.rearrange("(c p) -> p c", p=P),
                             allow_slow_non_contiguous=True).then_inc(biases_in, 16)
            for n, w in ((1, W2), (2, W3)):
                sp.dma_start(w_raw[:, K + n], w.rearrange("(c p) d -> p c d", p=P))\
                  .then_inc(gcn_weights_in[n], 16)

            def one(i, k):
                if (n := here(i, -2)) is not None:
                    load_x(n, (k + 2) % ROUND)
                    load_adj_blocks(n, (k + 2) % ROUND)
                if (n := here(i, LAG_D)) is not None:
                    store(n, (k - LAG_D) % ROUND)

            rounds(sp, one)
            for k in range(ROUND):
                sp.wait_ge(stored[k], 16 * (N_PAIRS // ROUND))

        @block.gpsimd
        def _(pool):
            pool.memset(ident[:], 0.0).then_inc(ident_zero, 1)
            pool.memset(minus_half[:], -0.5).then_inc(exponent_made, 1)
            for slot in p2:
                for part, value in zip(slot, (1.0, 0.0)):
                    pool.memset(plain(part[:, :, D:D + 2]), value).then_inc(ones_made, 1)
            pool.wait_ge(ident_zero, 1)
            pool.affine_select(out=ident[:], in_=ident[:], compare_op=ALU.not_equal, fill=1.0, base=0,
                               pattern=[[-1, P]], channel_multiplier=1).then_inc(ident_made, 1)
            pool.wait_ge(exponent_made, 1)

            def power(n, i, k):
                pool.wait_ge(veps_made[n], i + 1)
                if after(i, 2):
                    pool.wait_ge(norm_made[n], i - 1)
                pool.tensor_tensor(rstd[n][k % 2][:], veps[n][k % 2][:], minus_half[:], ALU.pow)\
                    .then_inc(rstd_made[n], 1)

            def y_low(n, i, k):
                if after(i, 1):
                    pool.wait_ge((s2_done, s3_done)[n], i)
                for c in range(C):
                    pool.wait_ge(y_made[n], C * i + c + 1)
                    pool.tensor_tensor(y[n][1][:, c], y_full[n][:, c], plain(y[n][0][:, c]), ALU.subtract)\
                        .then_inc(y_lo[n], 1)

            def out_bias(i, k):
                pool.wait_ge(x1_made, i + 1)
                if first(i):
                    pool.wait_ge(biases_in, 16 * BIAS_LOADS)
                if after(i, 4):
                    pool.wait_ge(out_made, i - 3)
                pool.tensor_tensor(x1b[k][:], x1[k % 2][:], bias_out[:], ALU.add).then_inc(x1b_made, 1)

            def adjT_low(i, k):
                pool.wait_ge(adjT_hi, i + 1)
                if after(i, 4):
                    pool.wait_ge(z_done[2], i - 3)
                pool.tensor_tensor(adjT[k][1][:], adjT_full[k][:], plain(adjT[k][0][:]), ALU.subtract)\
                    .then_inc(adjT_lo, 1)

            def k_weights_low(step, n, hi, lo, signal):
                pool.wait_ge(k_weights_hi, step)
                pool.tensor_tensor(lo, w_raw[:, n], plain(hi), ALU.subtract).then_inc(signal, 1)

            def gcn_weights_low():
                for n in range(K):
                    pool.wait_ge(gcn_weights_hi, n + 1)
                    pool.tensor_tensor(w_gcn[n][1][:], w_raw[:, K + n], plain(w_gcn[n][0][:]), ALU.subtract)\
                        .then_inc(gcn_weights_cut, 1)

            power(0, 0, 0)
            k_weights_low(1, 2, w_p2[0][:, :, 0:D], w_p2[1][:, :, 0:D], p2_weights_cut)
            for n in range(2):
                cols = slice(n * D, (n + 1) * D)
                k_weights_low(2 + n, n, w_p01[0][:, :, cols], w_p01[1][:, :, cols], p01_weights_cut)

            def sum_biases():
                pool.wait_ge(biases_in, 16 * BIAS_LOADS)
                pool.tensor_tensor(bias_part[:], bk_bc[:, 0, :], bk_bc[:, 1, :], ALU.add)\
                    .then_inc(bias_h_made, 1)
                pool.wait_ge(bias_h_made, 1)
                for g in range(G):
                    pool.tensor_tensor(bias_h[:, g, :], bias_part[:], bk_bc[:, 2, :], ALU.add)\
                        .then_inc(bias_h_made, 1)

            def one(i, k):
                b, c = here(i, LAG_B), here(i, LAG_C)
                if c is not None:
                    y_low(0, c, k - LAG_C)
                if b is not None:
                    power(1, b, k - LAG_B)
                    out_bias(b, (k - LAG_B) % ROUND)
                if (n := here(i, -1)) is not None:
                    power(0, n, k + 1)
                if first(i):
                    sum_biases()
                if c is not None:
                    y_low(1, c, k - LAG_C)
                if (n := here(i, 0)) is not None:
                    adjT_low(n, k)
                if first(i):
                    gcn_weights_low()

            rounds(pool, one)

        @block.scalar
        def _(act):
            act.dma_start(wv_raw[:], Wv.rearrange("(c p) d -> p c d", p=P)).then_inc(score_weights_in, 16)
            for n, landing in ((2, p2_weights_in), (0, p01_weights_in), (1, p01_weights_in)):
                act.dma_start(w_raw[:, n], Wk[n].rearrange("(c p) d -> p c d", p=P)).then_inc(landing, 16)

            act.wait_ge(p2_weights_in, 16)
            act.activation(w_p2[0][:, :, 0:D], w_raw[:, 2], ACT.Copy).then_inc(k_weights_hi, 1)

            def p01_weights_high():
                act.wait_ge(p01_weights_in, 16 * 2)
                for n in range(2):
                    act.activation(w_p01[0][:, :, n * D:(n + 1) * D], w_raw[:, n], ACT.Copy)\
                       .then_inc(k_weights_hi, 1)

            def hT_high(i, k):
                act.wait_ge(hT_done, i + 1)
                if after(i, 2):
                    act.wait_ge(p01_done, G * (i - 1))
                act.activation(h0T[k % 2][0][:], turned_ps, ACT.Relu).then_inc(hT_hi, 1)

            def adjT_high(i, k):
                act.wait_ge(adj_turned, i + 1)
                if after(i, 4):
                    act.wait_ge(z_done[2], i - 3)
                act.activation(adjT[k][0][:], adjT_full[k][:], ACT.Copy).then_inc(adjT_hi, 1)

            def scores_copy(i, k):
                act.wait_ge(p2_done, i + 1)
                if first(i):
                    act.wait_ge(half_c_made, 1)
                if after(i, 2):
                    act.wait_ge(spread_done, i - 1)
                    act.wait_ge(z_made, i - 1)
                act.activation(uv[k % 2][:], uv_ps, ACT.Identity, bias=half_c[:]).then_inc(uv_made, 1)

            def p2_high(i, k):
                if after(i, 2):
                    act.wait_ge(ap_done, i - 1)
                act.activation(p2[k % 2][0][:, :, 0:D], p2_ps, ACT.Copy).then_inc(p2_hi, 1)

            def logits(i, k):
                act.wait_ge(spread_done, i + 1)
                act.wait_ge(uv_made, i + 1)
                if after(i, 2):
                    act.wait_ge(exp_made, i - 1)
                act.activation(z[k % 2][:, 0, :], spread_ps[:, 0, :], ACT.Identity, bias=uv[k % 2][:, 0, 0:1])
                act.activation(z[k % 2][:, 1, :], spread_ps[:, 1, :], ACT.Identity, bias=uv[k % 2][:, 1, 0:1])\
                   .then_inc(z_made, 1)

            def exponentials(i, k):
                act.wait_ge(leaky_made, i + 1)
                if after(i, 2):
                    act.wait_ge(alpha_made, i - 1)
                act.activation(e[k % 2][:], z[k % 2][:], ACT.Exp).then_inc(exp_made, 1)

            def aT_high(i, k):
                act.wait_ge(alpha_made, i + 1)
                if after(i, 2):
                    act.wait_ge(ay_done, i - 1)
                act.activation(aT[k % 2][0][:], alpha[k % 2][:], ACT.Copy).then_inc(aT_hi, 1)

            def p1_copy(i, k, g):
                act.wait_ge(p01_done, G * i + g + 1)
                if g == 0 and after(i, 2):
                    act.wait_ge(y1_made, i - 1)
                act.activation(p1[k % 2][:, g], p1_ps[:, g], ACT.Copy).then_inc(p1_made, 1)

            def y1_high(i, k):
                act.wait_ge(y1_made, i + 1)
                if after(i, 2):
                    act.wait_ge(ay_done, i - 1)
                act.activation(y1[k % 2][0][:], y1_full[k % 2][:], ACT.Copy).then_inc(y1_hi, 1)

            def norm(i, k):
                act.wait_ge(shift_made, i + 1)
                if after(i, 2):
                    act.wait_ge(m_done, i - 1)
                for g in range(G):
                    last = act.activation(h1[k % 2][:, g, :], x1[k % 2][:, g, :], ACT.Relu,
                                          bias=nshift[k % 2][:, g:g + 1], scale=rstd[1][k % 2][:, g:g + 1])
                last.then_inc(norm_made[1], 1)

            def m_high(i):
                act.wait_ge(m_done, i + 1)
                if after(i, 1):
                    act.wait_ge(z_done[0], i)
                act.activation(m[0][:], turned_ps, ACT.Copy).then_inc(m_hi, 1)

            def s2_copy(i):
                act.wait_ge(s2_done, i + 1)
                if after(i, 1):
                    act.wait_ge(z_done[1], i)
                act.activation(s2[:], s2_ps, ACT.Copy).then_inc(s2_made, 1)

            def s3_high(i):
                act.wait_ge(s3_done, i + 1)
                if after(i, 1):
                    act.wait_ge(z_done[2], i)
                act.activation(s3[0][:], s3_ps, ACT.Copy).then_inc(s3_hi, 1)

            def gcn_weights_high():
                for n in range(K):
                    act.wait_ge(gcn_weights_in[n], 16)
                    act.activation(w_gcn[n][0][:], w_raw[:, K + n], ACT.Copy).then_inc(gcn_weights_hi, 1)

            def layer_result(n, i):
                act.wait_ge(z_done[n], i + 1)
                if first(i):
                    act.wait_ge(biases_in, 16 * BIAS_LOADS)
                if after(i, 1):
                    act.wait_ge(y_lo[n], C * i)
                    act.wait_ge((s2_done, s3_done)[n], i)
                for c in range(C):
                    for dst, made in ((y[n][0], y_hi[n]), (y_full[n], y_made[n])):
                        act.activation(dst[:, c], (z1_ps, z2_ps)[n][:, c], ACT.Relu,
                                       bias=bias_col[n][:, c:c + 1]).then_inc(made, 1)

            def one(i, k):
                a, b, c = here(i, 0), here(i, LAG_B), here(i, LAG_C)
                kb = (k - LAG_B) % ROUND
                if a is not None:
                    hT_high(a, k)
                if first(i):
                    p01_weights_high()
                if second(i):
                    gcn_weights_high()
                if c is not None:
                    layer_result(0, c)
                if tail(i - 1):
                    s3_high(here(i, LAG_D))
                if a is not None:
                    scores_copy(a, k)
                    p2_high(a, k)
                    logits(a, k)
                if c is not None:
                    s2_copy(c)
                if a is not None:
                    exponentials(a, k)
                    p1_copy(a, k, 0)
                if b is not None:
                    norm(b, kb)
                if a is not None:
                    aT_high(a, k)
                if c is not None:
                    layer_result(1, c)
                if a is not None:
                    p1_copy(a, k, 1)
                if b is not None:
                    m_high(b)
                if c is not None and not tail(i):
                    s3_high(c)
                if a is not None:
                    y1_high(a, k)
                    adjT_high(a, k)

            rounds(act, one)


        @block.vector
        def _(dve):
            def low(dst, src, hi, signal):
                dve.tensor_tensor(dst, src, plain(hi), ALU.subtract).then_inc(signal, 1)

            def statistics(n, i, k, src):
                if after(i, 2):
                    dve.wait_ge(mv_made[n], i - 1)
                for g in range(G):
                    last = dve.bn_stats(stats[n][k % 2][:, g, :], src[:, g, :])
                last.then_inc(stats_made[n], 1)

            def moments(n, i, k, between):
                dve.wait_ge(stats_made[n], i + 1)
                if after(i, 2):
                    dve.wait_ge((norm_made[0], shift_made)[n], i - 1)
                between()
                for g in range(G):
                    last = dve.bn_aggr(mv[n][k % 2][:, g, :], stats[n][k % 2][:, g, :])
                last.then_inc(mv_made[n], 1)

            def guard_variance(n, i, k):
                dve.wait_ge(mv_made[n], i + 1)
                if after(i, 2):
                    dve.wait_ge(rstd_made[n], i - 1)
                dve.tensor_scalar(veps[n][k % 2][:], mv[n][k % 2][:, :, 1], LN_EPS, None, ALU.add)\
                   .then_inc(veps_made[n], 1)

            def x_statistics(i, k):
                dve.wait_ge(x_landed[k], landed(i, k))
                statistics(0, i, k, x_in[k])

            def x_norm(i, k):
                dve.wait_ge(rstd_made[0], i + 1)
                if after(i, 2):
                    dve.wait_ge(hT_done, i - 1)
                for g in range(G):
                    last = dve.tensor_scalar(n0[k % 2][:, g, :], x_in[k][:, g, :], mv[0][k % 2][:, g, 0:1],
                                             rstd[0][k % 2][:, g:g + 1], ALU.subtract, ALU.mult)
                last.then_inc(norm_made[0], 1)

            def shift(i, k):
                dve.wait_ge(rstd_made[1], i + 1)
                if after(i, 2):
                    dve.wait_ge(norm_made[1], i - 1)
                dve.scalar_tensor_tensor(nshift[k % 2][:], mv[1][k % 2][:, :, 0], -1.0, rstd[1][k % 2][:],
                                         ALU.mult, ALU.mult).then_inc(shift_made, 1)

            def hT_low(i, k):
                hi, lo = h0T[k % 2]
                dve.wait_ge(hT_hi, i + 1)
                if after(i, 2):
                    dve.wait_ge(p01_done, G * (i - 1))
                dve.scalar_tensor_tensor(lo[:], turned_ps, 0.0, plain(hi[:]), ALU.max, ALU.subtract)\
                   .then_inc(hT_lo, 1)

            def turn_adj(i, k):
                dve.wait_ge(blocks_landed[k], landed(i, k) * (P // SQUARE))
                if after(i, 4):
                    dve.wait_ge(z_done[1], i - 3)
                    dve.wait_ge(adjT_lo, i - 3)
                dve.transpose(adjT_full[k][:].rearrange("p g m -> p (g m)"),
                              adj_blocks[k][:].rearrange("p g m -> p (g m)")).then_inc(adj_turned, 1)

            def p2_low(i, k):
                dve.wait_ge(p2_hi, i + 1)
                if after(i, 2):
                    dve.wait_ge(ap_done, i - 1)
                low(p2[k % 2][1][:, :, 0:D], p2_ps, p2[k % 2][0][:, :, 0:D], p2_lo)

            def leaky(i, k):
                dve.wait_ge(z_made, i + 1)
                zz = z[k % 2][:]
                dve.scalar_tensor_tensor(zz, zz, SLOPE, zz, ALU.mult, ALU.max).then_inc(leaky_made, 1)

            def attention(i, k):
                dve.wait_ge(exp_made, i + 1)
                dve.wait_ge(adj_turned, i + 1)
                if after(i, 2):
                    dve.wait_ge(aT_hi, i - 1)
                    dve.wait_ge(aT_lo, i - 1)
                dve.scalar_tensor_tensor(alpha[k % 2][:], adjT_full[k][:], HEADROOM, e[k % 2][:],
                                         ALU.mult, ALU.mult).then_inc(alpha_made, 1)

            def aT_low(i, k):
                dve.wait_ge(aT_hi, i + 1)
                if after(i, 2):
                    dve.wait_ge(ay_done, i - 1)
                low(aT[k % 2][1][:], alpha[k % 2][:], aT[k % 2][0][:], aT_lo)

            def guard_sum(i, k):
                dve.wait_ge(ap_done, i + 1)
                if after(i, 2):
                    dve.wait_ge(rinv_made, i - 1)
                dve.tensor_scalar(sums[k % 2][:], sums_ps, DIV_EPS * HEADROOM, None, ALU.add)\
                   .then_inc(sum_guarded, 1)

            def invert_sum(i, k):
                dve.wait_ge(sum_guarded, i + 1)
                if after(i, 2):
                    dve.wait_ge(h_made, i - 1)
                dve.reciprocal(rinv[k % 2][:], sums[k % 2][:]).then_inc(rinv_made, 1)

            def y1_sum(i, k):
                dve.wait_ge(rinv_made, i + 1)
                dve.wait_ge(p1_made, G * (i + 1))
                if after(i, 2):
                    dve.wait_ge(y1_lo, i - 1)
                for g in range(G):
                    last = dve.scalar_tensor_tensor(y1_full[k % 2][:, g, :], p2_ps[:, g, :],
                                                    rinv[k % 2][:, g:g + 1], p1[k % 2][:, g, :],
                                                    ALU.mult, ALU.add)
                last.then_inc(y1_made, 1)

            def y1_low(i, k):
                dve.wait_ge(y1_hi, i + 1)
                if after(i, 2):
                    dve.wait_ge(ay_done, i - 1)
                low(y1[k % 2][1][:], y1_full[k % 2][:], y1[k % 2][0][:], y1_lo)

            def p0_bias(i, k):
                dve.wait_ge(p1_made, G * (i + 1))
                if first(i):
                    dve.wait_ge(bias_h_made, 1 + G)
                if after(i, 2):
                    dve.wait_ge(h_made, i - 1)
                dve.tensor_tensor(p0b[k % 2][:], p0_ps, bias_h[:], ALU.add).then_inc(p0b_made, 1)

            def h_sum(i, k):
                dve.wait_ge(ay_done, i + 1)
                dve.wait_ge(p0b_made, i + 1)
                if after(i, 2):
                    dve.wait_ge(x1_made, i - 1)
                for g in range(G):
                    last = dve.scalar_tensor_tensor(hb[k % 2][:, g, :], ay_ps[:, g, :],
                                                    rinv[k % 2][:, g:g + 1], p0b[k % 2][:, g, :],
                                                    ALU.mult, ALU.add)
                last.then_inc(h_made, 1)

            def residual(i, k):
                dve.wait_ge(h_made, i + 1)
                if after(i, 2):
                    dve.wait_ge(x1b_made, i - 1)
                    dve.wait_ge(norm_made[1], i - 1)
                dve.scalar_tensor_tensor(x1[k % 2][:], hb[k % 2][:], 0.0, x_in[k][:], ALU.max, ALU.add)\
                   .then_inc(x1_made, 1)

            def x1_statistics(i, k):
                dve.wait_ge(x1_made, i + 1)
                statistics(1, i, k, x1[k % 2])

            def m_low(i):
                dve.wait_ge(m_hi, i + 1)
                if after(i, 1):
                    dve.wait_ge(z_done[0], i)
                low(m[1][:], turned_ps, m[0][:], m_lo)

            def s3_low(i):
                dve.wait_ge(s3_hi, i + 1)
                if after(i, 1):
                    dve.wait_ge(z_done[2], i)
                low(s3[1][:], s3_ps, s3[0][:], s3_lo)

            def finish(i, k):
                dve.wait_ge(z_done[2], i + 1)
                dve.wait_ge(x1b_made, i + 1)
                if after(i, 4):
                    dve.wait_ge(stored[k], landed(i - ROUND, k))
                dve.tensor_tensor(x_out[k][:], z3_ps, x1b[k][:], ALU.add).then_inc(out_made, 1)

            def dot(dst, a, b, junk, signal):
                dve.tensor_tensor_reduce(scratch[:, junk, :], a, b, 1.0, 0.0, ALU.mult, ALU.add, dst)\
                   .then_inc(signal, 1)

            def score_constant():
                dve.wait_ge(score_consts_in, 16 * 2)
                for h in range(2):
                    dot(bva[:, h:h + 1], bv_bc[:], aw_bc[:, h, :], 4 + h, bva_made)
                dve.wait_ge(bva_made, 2)
                dve.tensor_tensor(c_sum[:, 0:1], bva[:, 0:1], bva[:, 1:2], ALU.add).then_inc(c_summed, 1)
                dve.wait_ge(c_summed, 1)
                dve.tensor_tensor(c_sum[:, 1:2], c_sum[:, 0:1], ab_bc[:], ALU.add).then_inc(c_summed, 1)
                dve.wait_ge(c_summed, 2)
                dve.tensor_scalar(half_c[:], c_sum[:, 1:2], 0.5, None, ALU.mult).then_inc(half_c_made, 1)

            x_statistics(0, 0)
            moments(0, 0, 0, lambda: None)
            guard_variance(0, 0, 0)
            x_norm(0, 0)
            dve.wait_ge(score_weights_in, 16 * 2)
            for c in range(C):
                for h in range(2):
                    dot(wva[:, c, h:h + 1], wv_raw[:, c, :], aw_bc[:, h, :], 2 * c + h, wva_made)
            dve.wait_ge(wva_made, 2 * C)
            dve.tensor_copy(w_p2[0][:, :, D:D + 2], wva[:]).then_inc(score_columns_hi, 1)
            dve.wait_ge(score_columns_hi, 1)
            low(w_p2[1][:, :, D:D + 2], wva[:], w_p2[0][:, :, D:D + 2], p2_weights_cut)

            def first_round():
                hT_low(0, 0)
                score_constant()
                x_statistics(1, 1)
                turn_adj(0, 0)
                p2_low(0, 0)
                leaky(0, 0)
                moments(0, 1, 1, lambda: attention(0, 0))
                guard_variance(0, 1, 1)
                aT_low(0, 0)
                x_norm(1, 1)
                guard_sum(0, 0)
                invert_sum(0, 0)
                y1_sum(0, 0)
                y1_low(0, 0)
                p0_bias(0, 0)
                x_statistics(2, 2)

            def one(i, k):
                a, b, c, d = here(i, 0), here(i, LAG_B), here(i, LAG_C), here(i, LAG_D)
                nxt = here(i, -1)
                kb, kd, kn = (k - LAG_B) % ROUND, (k - LAG_D) % ROUND, (k + 1) % ROUND
                if first(i):
                    first_round()
                    return
                if tail(i - 1):
                    s3_low(d)
                if a is not None:
                    hT_low(a, k)
                if b is not None:
                    h_sum(b, kb)
                    residual(b, kb)
                    x1_statistics(b, kb)
                    moments(1, b, kb, lambda: p2_low(a, k) if a is not None else None)
                    guard_variance(1, b, kb)
                elif a is not None:
                    p2_low(a, k)
                if a is not None:
                    leaky(a, k)
                    turn_adj(a, k)
                if b is not None:
                    shift(b, kb)
                if nxt is not None:
                    moments(0, nxt, kn, lambda: attention(a, k))
                    guard_variance(0, nxt, kn)
                elif a is not None:
                    attention(a, k)
                if d is not None:
                    finish(d, kd)
                if a is not None:
                    aT_low(a, k)
                if nxt is not None:
                    x_norm(nxt, kn)
                if a is not None:
                    guard_sum(a, k)
                    invert_sum(a, k)
                if (n := here(i, -2)) is not None:
                    x_statistics(n, (k + 2) % ROUND)
                if a is not None:
                    y1_sum(a, k)
                if b is not None:
                    m_low(b)
                if c is not None and not tail(i):
                    s3_low(c)
                if a is not None:
                    y1_low(a, k)
                    p0_bias(a, k)

            rounds(dve, one)

        @block.tensor
        def _(pe):
            HI, LO = 0, 1
            PARTS = ((HI, HI), (HI, LO), (LO, HI))

            def matmul(dst, stationary, moving, start, stop):
                return pe.matmul(dst, stationary, moving, start=start, stop=stop, skip_group_check=True)

            def turn_h(i, k):
                pe.wait_ge(norm_made[0], i + 1)
                if after(i, 2):
                    pe.wait_ge(m_lo, i - 1)
                elif not first(i):
                    pe.wait_ge(hT_lo, i)
                for c in range(C):
                    for g in range(G):
                        last = pe.transpose(turned_ps[:, c, g, :], n0[k % 2][:, g, c * P:(c + 1) * P],
                                            ident[:])
                last.then_inc(hT_done, 1)

            def spread_scores(i, k):
                pe.wait_ge(uv_made, i + 1)
                if after(i, 1):
                    pe.wait_ge(h_made, i)
                for g in range(G):
                    last = pe.transpose(spread_ps[:, g, :], uv[k % 2][:, g, 1:2].to_broadcast([P, P]),
                                        ident[:])
                last.then_inc(spread_done, 1)

            def times_weights(hT, w, dst, starts, lo_wait):
                steps = [(g, c, a, b) for low in (False, True) for g in range(G) for c in range(C)
                         for a, b in PARTS if (a == LO) == low]
                for n, (g, c, a, b) in enumerate(steps):
                    if a == LO and steps[n - 1][2] == HI:
                        lo_wait()
                    start = c == 0 and a == HI and b == HI and g in starts
                    last = matmul(dst[g], hT[a][:, c, g, :], w[b][:, c, :], start, a == LO and c == C - 1)
                return last

            def p2_product(i, k):
                pe.wait_ge(hT_hi, i + 1)
                if first(i):
                    pe.wait_ge(p2_weights_cut, 2)
                if after(i, 1):
                    pe.wait_ge(y1_made, i)
                times_weights(h0T[k % 2], w_p2, [bank_p2[:, g, 0:D + 2] for g in range(G)], range(G),
                              lambda: pe.wait_ge(hT_lo, i + 1)).then_inc(p2_done, 1)

            def p01_product(i, k, g, chunks=range(C)):
                if g == 0 and first(i):
                    pe.wait_ge(p01_weights_cut, 2)
                if g == 0 and after(i, 1):
                    pe.wait_ge(p0b_made, i)
                    pe.wait_ge(p1_made, G * i)
                for c in chunks:
                    for a, b in PARTS:
                        last = matmul(bank_p[:, g, :], h0T[k % 2][a][:, c, g, :], w_p01[b][:, c, :],
                                      c == 0 and (a, b) == (HI, HI), c == C - 1 and a == LO)
                if C - 1 in chunks:
                    last.then_inc(p01_done, 1)

            def ap_product(i, k):
                if first(i):
                    pe.wait_ge(ones_made, 2 * 2)
                pe.wait_ge(aT_hi, i + 1)
                pe.wait_ge(p2_lo, i + 1)
                for a, b in PARTS:
                    if a == LO:
                        pe.wait_ge(aT_lo, i + 1)
                    for g in range(G):
                        last = matmul(bank_p2[:, g, 0:D + 2], aT[k % 2][a][:, g, :], p2[k % 2][b][:, g, :],
                                      (a, b) == (HI, HI), a == LO)
                last.then_inc(ap_done, 1)

            def ay_product(i, k):
                pe.wait_ge(y1_lo, i + 1)
                pe.wait_ge(z_made, i + 1)
                for g in range(G):
                    for a, b in PARTS:
                        last = matmul(ay_ps[:, g, :], aT[k % 2][a][:, g, :], y1[k % 2][b][:, g, :],
                                      g == 0 and (a, b) == (HI, HI), a == LO)
                last.then_inc(ay_done, 1)

            def aggregate(dst, src, i, k):
                for g in range(G):
                    for c in range(C):
                        last = matmul(dst[:, c, g, :], src[:, g, c * P:(c + 1) * P],
                                      adjT_full[k][:, g, :], g == 0 and c == 0, True)
                return last

            def m_product(i, k):
                pe.wait_ge(norm_made[1], i + 1)
                pe.wait_ge(adj_turned, i + 1)
                if here(i, -LAG_B) is not None:
                    pe.wait_ge(hT_lo, i + LAG_B + 1)
                else:
                    pe.wait_ge(m_lo, i)
                aggregate(turned_ps, h1[k % 2], i, k).then_inc(m_done, 1)

            def z1_product(i):
                pe.wait_ge(m_hi, i + 1)
                if first(i):
                    pe.wait_ge(gcn_weights_cut, 1)
                if after(i, 1):
                    pe.wait_ge(y_made[1], C * i)
                steps = [(o, c, a, b) for low in (False, True) for o in range(C) for c in range(C)
                         for b, a in PARTS if (b == LO) == low]
                for n, (o, c, a, b) in enumerate(steps):
                    if b == LO and steps[n - 1][3] == HI:
                        pe.wait_ge(m_lo, i + 1)
                    last = matmul(z1_ps[:, o], w_gcn[0][a][:, c, o * P:(o + 1) * P], m[b][:, c],
                                  n == 0, b == LO and c == C - 1)
                last.then_inc(z_done[0], 1)

            def s2_product(i):
                if first(i):
                    pe.wait_ge(gcn_weights_cut, 2)
                pe.wait_ge(y_made[0], C * (i + 1))
                times_weights(y[0], w_gcn[1], [s2_ps[:, g, :] for g in range(G)], (0,),
                              lambda: pe.wait_ge(y_lo[0], C * (i + 1))).then_inc(s2_done, 1)

            def z2_product(i, k):
                pe.wait_ge(s2_made, i + 1)
                aggregate(z2_ps, s2, i, k).then_inc(z_done[1], 1)

            def s3_product(i):
                if first(i):
                    pe.wait_ge(gcn_weights_cut, 3)
                pe.wait_ge(y_hi[1], C * (i + 1))
                if after(i, 1):
                    pe.wait_ge(out_made, i)
                times_weights(y[1], w_gcn[2], [s3_ps[:, g, :] for g in range(G)], (0,),
                              lambda: pe.wait_ge(y_lo[1], C * (i + 1))).then_inc(s3_done, 1)

            def z3_product(i, k):
                pe.wait_ge(s3_lo, i + 1)
                pe.wait_ge(adjT_lo, i + 1)
                for g in range(G):
                    for a, b in PARTS:
                        last = matmul(z3_ps[:, g, :], adjT[k][a][:, g, :], s3[b][:, g, :],
                                      g == 0 and (a, b) == (HI, HI), (a, b) == (LO, HI))
                last.then_inc(z_done[2], 1)

            unused = bank_p2[:, 0, 0:P]

            def keep_busy(count, dst=bank_3[:, 0:P]):
                for _ in range(count):
                    pe.transpose(dst, ident[:], ident[:])

            pe.wait_ge(ident_made, 1)
            keep_busy(BUSY_BEFORE)

            def one(i, k):
                a, b, c, d = here(i, 0), here(i, LAG_B), here(i, LAG_C), here(i, LAG_D)
                kb, kc, kd = (k - LAG_B) % ROUND, (k - LAG_C) % ROUND, (k - LAG_D) % ROUND
                if a is not None:
                    turn_h(a, k)
                if first(i):
                    keep_busy(BUSY_BETWEEN)
                if second(i):
                    keep_busy(BUSY_SECOND)
                if d is not None and not tail(i - 1):
                    z3_product(d, kd)
                if b is not None:
                    ay_product(b, kb)
                if a is not None:
                    p2_product(a, k)
                if c is not None:
                    s2_product(c)
                if tail(i - 1):
                    z3_product(d, kd)
                if a is not None:
                    spread_scores(a, k)
                    p01_product(a, k, 0)
                    p01_product(a, k, 1, (0,))
                if c is not None:
                    z2_product(c, kc)
                if a is not None:
                    p01_product(a, k, 1, (1,))
                    ap_product(a, k)
                if b is not None and tail(i):
                    keep_busy(BUSY_TAIL, unused)
                if b is not None:
                    m_product(b, kb)
                if b is not None and tail(i):
                    keep_busy(BUSY_TAIL // 2, unused)
                    z1_product(b)
                if c is not None:
                    s3_product(c)
                if b is not None and not tail(i):
                    z1_product(b)

            rounds(pe, one)


_OUT = "x_new"


def kernel(**inputs):
    import numpy as np
    import concourse.bacc as bacc
    from concourse.bass_utils import run_bass_kernel_spmd

    nc = bacc.Bacc("TRN2", target_bir_lowering=False, num_devices=1)
    arrays, args = {}, []
    for name in ("x", "adj", *("L0_gnn_" + n for n in ("Wv", "bv", "aw", "ab", "Wk", "bk")),
                 *("L1_gnn_" + n for n in ("W1", "b1", "W2", "b2", "W3", "b3"))):
        a = np.ascontiguousarray(inputs[name])
        arrays["in_" + name] = a
        args.append(nc.dram_tensor("in_" + name, a.shape, mybir.dt.from_np(a.dtype), kind="ExternalInput").ap())
    args.append(nc.dram_tensor(_OUT, inputs["x"].shape, F32, kind="ExternalOutput").ap())
    gnn_kernel(nc, *args)
    return run_bass_kernel_spmd(nc, [arrays], core_ids=[0]).results[0][_OUT]
```
